# Optimizing a Trainium2 kernel written in Bass

```python
import numpy as np
import jax
import jax.numpy as jnp

def _softmax(x, axis=-1):
    return jax.nn.softmax(x, axis=axis)

def _gelu(x):
    return jax.nn.gelu(x, approximate=True)

def _silu(x):
    return jax.nn.silu(x)

def _sigmoid(x):
    return jax.nn.sigmoid(x)

def _layernorm(x, axis=-1, eps=1e-05):
    m = jnp.mean(x, axis=axis, keepdims=True)
    v = jnp.var(x, axis=axis, keepdims=True)
    return (x - m) / jnp.sqrt(v + eps)

def _scatter_add(tgt, idx, src, axis=0):
    return tgt.at[idx].add(src)

def _segment_sum(src, seg, n):
    return jax.ops.segment_sum(src, seg, n)
kernel_name = 'mk_xattn_ffn_d1_seqx_r4_b64dce'

def setup_inputs(seed: int=0):
    np.random.seed(seed)
    _w = jnp.asarray

    def _rec_inputs():
        import jax
        import jax.numpy as jnp
        _rk = jax.random.key(seed)
        x = -0.0002928 + 1 * jax.random.normal(jax.random.fold_in(_rk, 1), (8, 512, 256), jnp.float32)
        _lenS = 512 - jax.random.randint(jax.random.fold_in(_rk, 7), (8,), 0, max(1, 512 // 4) + 1, jnp.int32)
        _lenS2 = 512 - jax.random.randint(jax.random.fold_in(_rk, 8), (8,), 0, max(1, 512 // 4) + 1, jnp.int32)
        _ctx_1024P = jax.random.normal(jax.random.fold_in(_rk, 11), (8, 16, 256), jnp.float32)
        _ctx_1024c = jax.random.dirichlet(jax.random.fold_in(_rk, 511), 0.3 * jnp.ones((16,), jnp.float32), (8, 512))
        _ctx_1024t = jnp.einsum('bsk,bkd->bsd', _ctx_1024c, _ctx_1024P)
        _ctx_1024t = _ctx_1024t * jax.lax.rsqrt(jnp.mean(jnp.square(_ctx_1024t)) + 1e-12) * 0.953939
        ctx_1024 = -1.39393e-06 + 0.999914 * (_ctx_1024t + 0.3 * jax.random.normal(jax.random.fold_in(_rk, 611), (8, 512, 256), jnp.float32))
        return (x, ctx_1024)
    x, ctx_1024 = _rec_inputs()

    def _L0_xattn_setup():
        import jax, jax.numpy as jnp
        import numpy as np
        import math
        NUM_HEADS = 16
        SIZE = 256
        HEAD_SIZE = SIZE // NUM_HEADS
        B, S = (2, 512)

        def _split_heads(x):
            b, s, _ = x.shape
            return x.reshape(b, s, NUM_HEADS, HEAD_SIZE).transpose(0, 2, 1, 3)
        key = jax.random.key(seed)
        ks = jax.random.split(key, 11)
        sc = 1.0 / math.sqrt(SIZE)
        inp = {'q': jax.random.normal(ks[0], (B, S, SIZE), dtype=jnp.float32), 'k': jax.random.normal(ks[1], (B, S, SIZE), dtype=jnp.float32), 'v': jax.random.normal(ks[2], (B, S, SIZE), dtype=jnp.float32), 'Wq': jax.random.normal(ks[3], (SIZE, SIZE), dtype=jnp.float32) * sc, 'bq': jax.random.normal(ks[4], (SIZE,), dtype=jnp.float32) * sc, 'Wk': jax.random.normal(ks[5], (SIZE, SIZE), dtype=jnp.float32) * sc, 'bk': jax.random.normal(ks[6], (SIZE,), dtype=jnp.float32) * sc, 'Wv': jax.random.normal(ks[7], (SIZE, SIZE), dtype=jnp.float32) * sc, 'bv': jax.random.normal(ks[8], (SIZE,), dtype=jnp.float32) * sc, 'Wo': jax.random.normal(ks[9], (SIZE, SIZE), dtype=jnp.float32) * sc, 'bo': jax.random.normal(ks[10], (SIZE,), dtype=jnp.float32) * sc}
        return inp
    _L0_xattn_all = _L0_xattn_setup()
    _L0_xattn_in = {k: v for k, v in _L0_xattn_all.items() if k in ('Wq', 'bq', 'Wk', 'bk', 'Wv', 'bv', 'Wo', 'bo')}
    del _L0_xattn_all

    def _L0_ffn_setup():
        import jax, jax.numpy as jnp
        import numpy as np
        NUM_GEMMS = 8
        HIDDEN = 256
        INTER = 1024
        key = jax.random.key(seed)
        k_x, k_w1, k_b1, k_w2, k_b2 = jax.random.split(key, 5)
        x = jax.random.normal(k_x, (8, 512, HIDDEN), dtype=jnp.float32)
        s1 = 1.0 / np.sqrt(HIDDEN)
        s2 = 1.0 / np.sqrt(INTER)
        W1 = jax.random.uniform(k_w1, (NUM_GEMMS, INTER, HIDDEN), jnp.float32, -s1, s1)
        b1 = jax.random.uniform(k_b1, (NUM_GEMMS, INTER), jnp.float32, -s1, s1)
        W2 = jax.random.uniform(k_w2, (NUM_GEMMS, HIDDEN, INTER), jnp.float32, -s2, s2)
        b2 = jax.random.uniform(k_b2, (NUM_GEMMS, HIDDEN), jnp.float32, -s2, s2)
        return {'x': x, 'W1': W1, 'b1': b1, 'W2': W2, 'b2': b2}
    _L0_ffn_all = _L0_ffn_setup()
    _L0_ffn_in = {k: v for k, v in _L0_ffn_all.items() if k in ('W1', 'b1', 'W2', 'b2')}
    del _L0_ffn_all
    return {'x': x, 'ctx_1024': ctx_1024, 'L0_xattn_Wq': _L0_xattn_in['Wq'], 'L0_xattn_bq': _L0_xattn_in['bq'], 'L0_xattn_Wk': _L0_xattn_in['Wk'], 'L0_xattn_bk': _L0_xattn_in['bk'], 'L0_xattn_Wv': _L0_xattn_in['Wv'], 'L0_xattn_bv': _L0_xattn_in['bv'], 'L0_xattn_Wo': _L0_xattn_in['Wo'], 'L0_xattn_bo': _L0_xattn_in['bo'], 'L0_ffn_W1': _L0_ffn_in['W1'], 'L0_ffn_b1': _L0_ffn_in['b1'], 'L0_ffn_W2': _L0_ffn_in['W2'], 'L0_ffn_b2': _L0_ffn_in['b2']}

def reference(x, ctx_1024, L0_xattn_Wq, L0_xattn_bq, L0_xattn_Wk, L0_xattn_bk, L0_xattn_Wv, L0_xattn_bv, L0_xattn_Wo, L0_xattn_bo, L0_ffn_W1, L0_ffn_b1, L0_ffn_W2, L0_ffn_b2):
    import jax
    import jax.numpy as jnp

    def _L0_xattn_ref(q, k, v, Wq, bq, Wk, bk, Wv, bv, Wo, bo):
        import jax, jax.numpy as jnp
        import numpy as np
        import math
        NUM_HEADS = 16
        SIZE = 256
        HEAD_SIZE = SIZE // NUM_HEADS
        B, S = (2, 512)

        def _split_heads(x):
            b, s, _ = x.shape
            return x.reshape(b, s, NUM_HEADS, HEAD_SIZE).transpose(0, 2, 1, 3)
        qh = _split_heads(q @ Wq.T + bq) / math.sqrt(HEAD_SIZE)
        kh = _split_heads(k @ Wk.T + bk)
        vh = _split_heads(v @ Wv.T + bv)
        scores = jnp.einsum('bhqd,bhkd->bhqk', qh, kh)
        attn = jax.nn.softmax(scores, axis=-1)
        ctx = jnp.einsum('bhqk,bhkd->bhqd', attn, vh)
        ctx = ctx.transpose(0, 2, 1, 3).reshape(q.shape[0], -1, SIZE)
        return ctx @ Wo.T + bo

    def _L0_ffn_ref(x, W1, b1, W2, b2):
        import jax, jax.numpy as jnp
        import numpy as np
        NUM_GEMMS = 8
        HIDDEN = 256
        INTER = 1024
        orig_shape = x.shape
        token_num = int(np.prod(orig_shape[:-1]))
        m = token_num // NUM_GEMMS
        xg = x.reshape(NUM_GEMMS, m, HIDDEN)
        h1 = jnp.einsum('gmh,goh->gmo', xg, W1) + b1[:, None, :]
        h2 = jnp.einsum('gmo,gho->gmh', h1, W2) + b2[:, None, :]
        return h2.reshape(orig_shape)
    x = x + _L0_xattn_ref(_layernorm(x, axis=-1), ctx_1024, ctx_1024, L0_xattn_Wq, L0_xattn_bq, L0_xattn_Wk, L0_xattn_bk, L0_xattn_Wv, L0_xattn_bv, L0_xattn_Wo, L0_xattn_bo)
    x = x + _L0_ffn_ref(_layernorm(x, axis=-1), L0_ffn_W1, L0_ffn_b1, L0_ffn_W2, L0_ffn_b2)
    return x

_drawn_inputs = setup_inputs


def setup_inputs(seed=0):
    import zlib

    import numpy as np

    out = dict(_drawn_inputs(seed))
    spreads = {}
    factors = {'L0_xattn_bq': 4.595, 'L0_xattn_bk': 8.0, 'L0_ffn_b1': 3.302, 'L0_ffn_b2': 3.791}
    for name, (base, spread) in spreads.items():
        noise = np.random.default_rng([zlib.crc32(name.encode()), seed]).standard_normal(out[name].shape)
        drawn = base * np.exp(spread * noise) if base else spread * noise
        out[name] = jnp.asarray(drawn.astype(out[name].dtype))
    for name, factor in factors.items():
        out[name] = (out[name] * factor).astype(out[name].dtype)
    return out
```

```python
from contextlib import ExitStack

import concourse.bass as bass
from concourse import mybir

F32 = mybir.dt.float32
F32R = mybir.dt.float32r
ALU = mybir.AluOpType
ACT = mybir.ActivationFunctionType
AX = mybir.AxisListType

P = 128
B = 8
S = 512
D = 256
H = 16
HD = D // H
INTER = 1024
C = S // P
F = D // P
OC = INTER // P
QUADS = H // 4
UNITS = QUADS * 16
LEAD = 24
EPS = 1e-5
SCALE = float(HD) ** -0.5
SLOTS = ((0, 0), (1, 0), (0, 1), (1, 1))
ZROW, MROW = 64, 96
KN, KS = MROW, MROW + 2
LAST = B - 1


def xattn_ffn(nc, x, ctxT, wqT, bq, wkT, bk, wvT, bv, woT, bo, w1, b1, w2T, b2, out):
    with ExitStack() as stack:
        def sb(name, shape, dt=F32):
            return stack.enter_context(nc.sbuf_tensor(name, shape, dt))

        def pb(name):
            return stack.enter_context(nc.psum_tensor(name, [P, S], F32))

        def sem(name):
            return stack.enter_context(nc.semaphore(name))

        ident = sb("ident", [P, P])
        ones = sb("ones", [P, P])
        half_lo = sb("half_lo", [P, 1])
        half_hi = sb("half_hi", [P, 1])
        neg_half = sb("neg_half", [P, C])
        wq_in = sb("wq_in", [P, F, D])
        wq = sb("wq", [P, F, D])
        wk = sb("wk", [P, F, D])
        wv = sb("wv", [P, F, D])
        wo = sb("wo", [P, F, D])
        bq_in = sb("bq_in", [P, 2])
        bqk = sb("bqk", [P, 2, 2])
        bv_all = sb("bv_all", [P, 2, D])
        bo_all = sb("bo_all", [P, D])
        x_in = sb("x_in", [P, C, D])
        x_bo_next = sb("x_bo_next", [P, C, D])
        x_bo = sb("x_bo", [P, C, D])
        ctx_in = sb("ctx_in", [P, F, S])
        normed = sb("normed", [P, C, D])
        normedT = sb("normedT", [P, F, S])
        stats = [sb(f"stats{i}", [P, C, 6]) for i in range(2)]
        mean_var = [sb(f"mean_var{i}", [P, C, 2]) for i in range(2)]
        var_eps = [sb(f"var_eps{i}", [P, C]) for i in range(2)]
        rstd = [sb(f"rstd{i}", [P, C]) for i in range(2)]
        hi = sb("hi", [P, 2, 2, S], F32R)
        lo = sb("lo", [P, 2, 2, S], F32R)
        qs = sb("qs", [P, H, S], F32R)
        ks = sb("ks", [P, H, S], F32R)
        v_nat = sb("v_nat", [P, C, D])
        vs = sb("vs", [P, C, H, 32])
        neg_max = sb("neg_max", [P, 2, 16])
        max_hi = sb("max_hi", [16, P], F32R)
        max_lo = sb("max_lo", [16, P], F32R)
        probs = [sb(f"probs{i}", [P, 4, S]) for i in range(2)]
        even_ctx = sb("even_ctx", [P, S])
        even_sum = sb("even_sum", [P, S])
        pair_ctx = sb("pair_ctx", [P, S])
        pair_sum = sb("pair_sum", [P, S])
        sum_here = sb("sum_here", [P, S])
        inv_sum = sb("inv_sum", [P, S])
        attnT = sb("attnT", [P, 2, S])
        y = sb("y", [P, C, D])
        y_b = sb("y_b", [P, C, D])
        res = sb("res", [P, C, D])
        w1_in = sb("w1_in", [P, OC, D])
        w2_in = sb("w2_in", [P, OC, D])
        b1_in = sb("b1_in", [P, OC])
        b2_in = sb("b2_in", [1, D])
        b2_part = sb("b2_part", [P, OC, D])
        b2_all = sb("b2_all", [P, D])
        w21 = sb("w21", [P, F, D])

        st_bank = [pb("st0"), pb("st1")]
        nat_bank = [pb("nat0"), pb("nat1")]
        pv_bank = [pb("pv0"), pb("pv1")]
        misc = [pb("misc0"), pb("misc1")]

        const_in = sem("const_in")
        x_loaded = sem("x_loaded")
        ctx_loaded = sem("ctx_loaded")
        ffn_loaded = sem("ffn_loaded")
        stacked = [sem(f"stacked{g}") for g in range(QUADS)]
        max_rows = sem("max_rows")
        stored = sem("stored")
        pool_set = sem("pool_set")
        dve_set = sem("dve_set")
        act_set = sem("act_set")
        st_done = sem("st_done")
        nat_done = sem("nat_done")
        pv_done = sem("pv_done")
        maxT_done = sem("maxT_done")
        xT_done = sem("xT_done")
        qk_done = sem("qk_done")
        v_done = sem("v_done")
        wo_done = sem("wo_done")
        b2_done = sem("b2_done")
        yT_done = sem("yT_done")
        z_done = sem("z_done")
        w21_done = sem("w21_done")
        exp_done = sem("exp_done")
        xT_ready = sem("xT_ready")
        yT_ready = sem("yT_ready")
        hi_ready = sem("hi_ready")
        even_out = sem("even_out")
        b2_ready = sem("b2_ready")
        w21_ready = sem("w21_ready")
        max_done = sem("max_done")
        lo_ready = sem("lo_ready")
        maxhi_ready = sem("maxhi_ready")
        max_ready = sem("max_ready")
        v_ready = sem("v_ready")
        odd_out = sem("odd_out")
        sum_ready = sem("sum_ready")
        y_ready = sem("y_ready")
        out_ready = sem("out_ready")
        stat_done = [sem("xstat_done"), sem("ystat_done")]
        aggr_done = [sem("xaggr_done"), sem("yaggr_done")]
        eps_done = [sem("xeps_done"), sem("yeps_done")]
        rstd_ready = [sem("xrstd_ready"), sem("yrstd_ready")]
        norm_ready = [sem("xnorm_ready"), sem("ynorm_ready")]
        v_stacked = sem("v_stacked")
        inv_ready = sem("inv_ready")
        attn_ready = sem("attn_ready")
        xbo_next_ready = sem("xbo_next_ready")
        xbo_ready = sem("xbo_ready")
        yb_ready = sem("yb_ready")
        b2_step = sem("b2_step")
        b2_part_ready = sem("b2_part_ready")

        passed = {e.engine: sem(f"passed_{n}") for e, n in
                  ((nc.sync, "sp"), (nc.vector, "dve"), (nc.gpsimd, "pool"))}

        CONSTS = 9 * 16

        def wait(eng, s, value):
            if not (isinstance(value, int) and value <= 0):
                eng.wait_ge(s, value)

        def wait_apart(eng, s, value):
            wait(eng, s, value)
            if not isinstance(value, int):
                eng.sem_inc(passed[eng.engine], 1)

        def turns(eng, turn):
            turn(0, False, True, True)
            turn(1, True, True, True)
            with eng.Fori(2, B - 2) as b:
                turn(b, True, True, True)
            turn(B - 2, True, True, False)
            turn(B - 1, True, False, False)

        block = stack.enter_context(nc.Block())

        @block.sync
        def _(sp):
            def load_x(b):
                sp.dma_start(x_in[:, :, :], x[b].rearrange("(p c) d -> p c d", c=C)).then_inc(x_loaded, 16)

            def load_ctx(b):
                sp.dma_start(ctx_in[:, :, :], ctxT[b].rearrange("f p s -> p f s")).then_inc(ctx_loaded, 16)

            def load_ffn(b):
                sp.dma_start(w1_in[:, :, :], w1[b].rearrange("(p o) d -> p o d", o=OC)).then_inc(ffn_loaded, 16)
                sp.dma_start(w2_in[:, :, :], w2T[b].rearrange("(p o) d -> p o d", o=OC)).then_inc(ffn_loaded, 16)
                sp.dma_start(b1_in[:, :], b1[b].rearrange("(p o) -> p o", o=OC)).then_inc(ffn_loaded, 16)
                sp.dma_start(b2_in[:, :], b2[b].rearrange("(a d) -> a d", a=1)).then_inc(ffn_loaded, 16)

            def stack_quad(b, g):
                wait_apart(sp, lo_ready, 4 * b + 2 * (g // 2) + 2)
                wait_apart(sp, st_done, UNITS * (b - 1) + 16 * g + 16)
                rows = slice(64 * (g % 2), 64 * (g % 2) + 64)
                for s, halves in enumerate(SLOTS):
                    for which, dst in ((0, qs), (1, ks)):
                        src = (hi, lo)[halves[which]]
                        sp.dma_start(dst[16 * s:16 * s + 16, 4 * g:4 * g + 4, :].bitcast(F32),
                                     src[rows, which, g // 2, :].bitcast(F32)).then_inc(stacked[g], 16)

            def store_max(b, g):
                wait_apart(sp, max_ready, 4 * b + g + 1)
                wait_apart(sp, st_done, UNITS * (b - 1) + 16 * g + 16)
                for r, src in enumerate((max_hi, max_lo)):
                    dst = qs[MROW + r:MROW + r + 1, 4 * g:4 * g + 4, :].bitcast(F32)
                    sp.dma_start(dst.rearrange("a h (c t) -> a (h c) t", c=C),
                                 src[:, :].bitcast(F32)).then_inc(max_rows, 16)

            def store_out(b, half):
                wait_apart(sp, out_ready, 2 * b + half + 1)
                sp.dma_start(out[b].rearrange("(p c) d -> p c d", c=C)[:, 2 * half:2 * half + 2, :],
                             res[:, 2 * half:2 * half + 2, :]).then_inc(stored, 16)

            def turn(b, post, prep, load):
                if post:
                    stack_quad(b, 3)
                    wait_apart(sp, w21_done, b)
                    wait_apart(sp, b2_part_ready, b)
                    load_ffn(b)
                store_max(b, 1)
                if prep:
                    stack_quad(b + 1, 0)
                store_max(b, 2)
                if prep:
                    stack_quad(b + 1, 1)
                if load:
                    wait_apart(sp, norm_ready[0], 4 * (b + 2))
                    wait_apart(sp, xbo_next_ready, b + 2)
                    load_x(b + 2)
                    wait_apart(sp, v_done, 2 * (b + 2))
                    wait_apart(sp, qk_done, 4 * (b + 2))
                    load_ctx(b + 2)
                if post:
                    store_out(b - 1, 0)
                    store_out(b - 1, 1)
                store_max(b, 3)
                if prep:
                    stack_quad(b + 1, 2)
                    store_max(b + 1, 0)

            load_x(0)
            sp.dma_start(wq_in[:, :, :], wqT.rearrange("(f p) d -> p f d", p=P)).then_inc(const_in, 16)
            sp.dma_start(bq_in[:, :], bq).then_inc(const_in, 16)
            load_ctx(0)
            sp.dma_start(wk[:, :, :], wkT.rearrange("(f p) d -> p f d", p=P)).then_inc(const_in, 16)
            sp.dma_start(bqk[:, 1, :], bk).then_inc(const_in, 16)
            sp.dma_start(wv[:, :, :], wvT.rearrange("(f p) d -> p f d", p=P)).then_inc(const_in, 16)
            for i in range(2):
                sp.dma_start(bv_all[:, i, :], bv.partition_broadcast(P)).then_inc(const_in, 16)
            sp.dma_start(bo_all[:, :], bo.partition_broadcast(P)).then_inc(const_in, 16)
            sp.dma_start(wo[:, :, :], woT.rearrange("(f p) d -> p f d", p=P)).then_inc(const_in, 16)
            load_ffn(0)
            sp.wait_ge(dve_set, 8)
            for g in range(QUADS):
                stack_quad(0, g)
                if g == 0:
                    sp.wait_ge(norm_ready[0], 4)
                    sp.wait_ge(xbo_next_ready, 1)
                    load_x(1)
                    sp.wait_ge(v_done, 2)
                    sp.wait_ge(qk_done, 4)
                    load_ctx(1)
            store_max(0, 0)
            turns(sp, turn)
            store_out(LAST, 0)
            store_out(LAST, 1)
            sp.wait_ge(stored, 32 * B)

        @block.tensor
        def _(pe):
            mm = nc.tensor.matmul

            def nat(b, n):
                g, j, c = n // 16, n % 16 // 4, n % 4
                h = 4 * g + j
                if n % 16 == 0:
                    wait(pe, stacked[g], 128 * (b + 1))
                wait(pe, max_done, UNITS * b + n - 1)
                mm(nat_bank[n % 2][:, :], qs[0:KN, h, c * P:(c + 1) * P], ks[0:KN, h, :],
                   start=True, stop=True).then_inc(nat_done, 1)

            def st(b, u):
                g, kc, j = u // 16, u % 16 // 4, u % 4
                h = 4 * g + j
                if u % 16 == 0:
                    wait(pe, max_rows, 32 * (4 * b + g + 1))
                wait(pe, exp_done, UNITS * b + u - 1)
                mm(st_bank[u % 2][:, :], ks[0:KS, h, kc * P:(kc + 1) * P], qs[0:KS, h, :],
                   start=True, stop=True).then_inc(st_done, 1)

            def pv(b, n):
                g, kc = n // 4, n % 4
                if kc == 0:
                    wait(pe, v_stacked, 4 * b + g + 1)
                    if g % 2 == 0:
                        wait(pe, even_out, 2 * (2 * b + g // 2))
                    else:
                        wait(pe, odd_out, 2 * (2 * b + g // 2))
                wait(pe, exp_done, UNITS * b + 4 * n + 4)
                for j in range(4):
                    last = mm(pv_bank[g % 2][32 * j:32 * j + 32, :], vs[:, kc, 4 * g + j, :],
                              probs[n % 2][:, j, :], start=(kc == 0), stop=(kc == 3),
                              tile_position=(0, 32 * j), skip_group_check=True)
                last.then_inc(pv_done, 1)

            def transposeT(bank, f, done):
                for c in range(C):
                    last = nc.tensor.transpose(misc[bank][:, c * P:(c + 1) * P],
                                               normed[:, c, f * P:(f + 1) * P], ident[:, :])
                last.then_inc(done, 1)

            def xT(b, f, bank):
                wait(pe, norm_ready[0], 4 * b + 4)
                transposeT(bank, f, xT_done)

            def yT(b, f, bank):
                wait(pe, norm_ready[1], 4 * b + 4)
                transposeT(bank, f, yT_done)

            def maxT(b, g, bank):
                wait(pe, max_done, UNITS * b + 16 * g + 16)
                nc.tensor.transpose(misc[bank][0:16, 0:P], neg_max[:, g % 2, :],
                                    ident[:, :]).then_inc(maxT_done, 1)

            def qk(b, i, bank, f):
                which, m = i % 2, i // 2
                if which == 0:
                    wait(pe, xT_ready, 2 * b + 2)
                src, w = (normedT, wq) if which == 0 else (ctx_in, wk)
                last = mm(misc[bank][:, :], w[:, f, m * P:(m + 1) * P], src[:, f, :],
                          start=(f == 0), stop=(f == F - 1))
                if f == F - 1:
                    last.then_inc(qk_done, 1)

            def v(b, c, bank):
                if c == 0:
                    wait(pe, ctx_loaded, 16 * (b + 1))
                for f in range(F):
                    last = mm(misc[bank][:, (c % 2) * D:(c % 2 + 1) * D], ctx_in[:, f, c * P:(c + 1) * P],
                              wv[:, f, :], start=(f == 0), stop=(f == F - 1))
                if c % 2:
                    last.then_inc(v_done, 1)

            def wo_(b, c, bank):
                if c == 0:
                    wait(pe, attn_ready, 2 * b + 2)
                for f in range(F):
                    last = mm(misc[bank][:, (c % 2) * D:(c % 2 + 1) * D], attnT[:, f, c * P:(c + 1) * P],
                              wo[:, f, :], start=(f == 0), stop=(f == F - 1))
                if c % 2:
                    last.then_inc(wo_done, 1)

            def b2sum(b, bank):
                wait(pe, b2_part_ready, b + 1)
                mm(misc[bank][:, 0:D], ones[:, :], b2_part[:, 0, :], start=True, stop=True).then_inc(b2_done, 1)

            def z(b, c, bank):
                if c == 0:
                    wait(pe, yT_ready, 2 * b + 2)
                    wait(pe, w21_ready, b + 1)
                for f in range(F):
                    last = mm(misc[bank][:, (c % 2) * D:(c % 2 + 1) * D], normedT[:, f, c * P:(c + 1) * P],
                              w21[:, f, :], start=(f == 0), stop=(f == F - 1))
                if c % 2:
                    last.then_inc(z_done, 1)

            def w21_part(b, n, bank):
                f, o = n // OC, n % OC
                if n == 0:
                    wait(pe, ffn_loaded, 64 * (b + 1))
                last = mm(misc[bank][:, f * D:(f + 1) * D], w1_in[:, o, f * P:(f + 1) * P], w2_in[:, o, :],
                          start=(o == 0), stop=(o == OC - 1))
                if n == F * OC - 1:
                    last.then_inc(w21_done, 1)

            def jobs(b, u, post, prep):
                if prep:
                    if u == 6:
                        wait(pe, w21_ready, b)
                        wait(pe, v_ready, 2 * b + 2)
                    if u in (6, 7):
                        v(b + 1, u - 6, 0)
                    if u == 8:
                        wait(pe, max_ready, 4 * b + 1)
                    if u in (8, 9):
                        v(b + 1, u - 6, 1)
                if u == 10:
                    wait(pe, v_ready, 2 * b + 3 if prep else 0)
                    wait(pe, w21_ready, b)
                    maxT(b, 1, 0)
                if prep:
                    if u == 11:
                        wait(pe, v_ready, 2 * b + 4)
                        xT(b + 1, 0, 1)
                    if u == 12:
                        wait(pe, max_ready, 4 * b + 2)
                        xT(b + 1, 1, 0)
                if post:
                    if u == 14:
                        wait(pe, xT_ready, 2 * b + 3 if prep else 0)
                        wait(pe, max_ready, 4 * b + 1)
                    if u in (14, 15):
                        wo_(b - 1, u - 14, 1)
                    if u == 16:
                        wait(pe, xT_ready, 2 * b + 4 if prep else 0)
                        wait(pe, max_ready, 4 * b + 2)
                    if u in (16, 17):
                        wo_(b - 1, u - 14, 0)
                if prep:
                    if u == 18:
                        wait(pe, y_ready, 2 * b - 1 if post else 0)
                    if u in (18, 19):
                        qk(b + 1, 0, 1, u - 18)
                    if u == 20:
                        wait(pe, y_ready, 2 * b if post else 0)
                    if u in (20, 21):
                        qk(b + 1, 1, 0, u - 20)
                    if u == 22:
                        wait(pe, lo_ready, 4 * b + 5)
                    if u in (22, 23):
                        qk(b + 1, 2, 1, u - 22)
                    if u == 24:
                        wait(pe, lo_ready, 4 * b + 6)
                    if u in (24, 25):
                        qk(b + 1, 3, 0, u - 24)
                if u == 26:
                    wait(pe, lo_ready, 4 * b + 7 if prep else 0)
                    wait(pe, y_ready, 2 * b - 1 if post else 0)
                    maxT(b, 2, 1)
                if post:
                    if u == 28:
                        wait(pe, lo_ready, 4 * b + 8 if prep else 0)
                        wait(pe, y_ready, 2 * b)
                        b2sum(b - 1, 0)
                    if u == 30:
                        wait(pe, max_ready, 4 * b + 3)
                        yT(b - 1, 0, 1)
                    if u == 31:
                        wait(pe, b2_ready, b)
                        yT(b - 1, 1, 0)
                    if u in (33, 34):
                        z(b - 1, u - 33, 1)
                    if u in (35, 36):
                        z(b - 1, u - 33, 0)
                if u == 42:
                    wait(pe, out_ready, 2 * b - 1 if post else 0)
                    wait(pe, max_ready, 4 * b + 3)
                    maxT(b, 3, 1)
                if u == 43:
                    wait(pe, out_ready, 2 * b if post else 0)
                    wait(pe, lo_ready, 4 * b + 8 if prep else 0)
                if 43 <= u < 59:
                    w21_part(b, u - 43, 0)
                if u == 59 and prep:
                    wait(pe, max_ready, 4 * b + 4)
                    maxT(b + 1, 0, 1)

            def turn(b, post, prep, load):
                for u in range(UNITS):
                    st(b, u)
                    n = u + LEAD
                    if n < UNITS:
                        nat(b, n)
                    elif prep:
                        nat(b + 1, n - UNITS)
                    if u % 4 == 2:
                        if u > 4:
                            pv(b, u // 4 - 1)
                        elif post:
                            pv(b - 1, 15)
                    jobs(b, u, post, prep)

            pe.wait_ge(pool_set, 3)
            pe.wait_ge(dve_set, 8)
            pe.wait_ge(act_set, 2)
            xT(0, 0, 1)
            xT(0, 1, 0)
            pe.wait_ge(const_in, CONSTS)
            pe.wait_ge(ctx_loaded, 16)
            for i, bank in enumerate((1, 0, 1, 0)):
                if i >= 2:
                    pe.wait_ge(lo_ready, i - 1)
                for f in range(F):
                    qk(0, i, bank, f)
            for c in range(C):
                if c % 2 == 0:
                    pe.wait_ge(lo_ready, 4 if c == 0 else 3)
                v(0, c, c // 2)
            for n in range(LEAD):
                nat(0, n)
                if n == 18:
                    pe.wait_ge(v_ready, 2)
                    maxT(0, 0, 1)
            turns(pe, turn)
            pv(LAST, 15)
            pe.wait_ge(max_ready, 4 * B)
            wo_(LAST, 0, 1)
            wo_(LAST, 1, 1)
            pe.wait_ge(w21_ready, B)
            wo_(LAST, 2, 0)
            wo_(LAST, 3, 0)
            pe.wait_ge(y_ready, 2 * B)
            b2sum(LAST, 0)
            yT(LAST, 0, 1)
            pe.wait_ge(b2_ready, B)
            yT(LAST, 1, 0)
            for c in range(C):
                z(LAST, c, 1 - c // 2)

        @block.scalar
        def _(act):
            def exp(b, u):
                kc, j = u // 4, u % 4
                wait(act, st_done, UNITS * b + u + 1)
                if j == 0:
                    wait(act, pv_done, 16 * b + kc - 1)
                act.activation(probs[kc % 2][:, j, :], st_bank[u % 2][:, :], ACT.Exp).then_inc(exp_done, 1)

            def xT_copy(b, f, bank):
                wait(act, xT_done, 2 * b + f + 1)
                wait(act, z_done, 2 * (b - 2))
                wait(act, qk_done, 4 * (b - 1) + 3)
                act.activation(normedT[:, f, :], misc[bank][:, :], ACT.Copy).then_inc(xT_ready, 1)

            def yT_copy(b, f, bank, prep):
                wait(act, yT_done, 2 * b + f + 1)
                wait(act, qk_done, 4 * (b + 2) + 3 if prep else 0)
                wait(act, z_done, 2 * b)
                act.activation(normedT[:, f, :], misc[bank][:, :], ACT.Copy).then_inc(yT_ready, 1)

            def hi_half(b, i, bank):
                which, m = i % 2, i // 2
                wait(act, qk_done, 4 * b + i + 1)
                for g in (2 * m, 2 * m + 1):
                    wait(act, stacked[g], 128 * b)
                act.activation(hi[:, which, m, :], misc[bank][:, :], ACT.Identity,
                               bias=bqk[:, which, m:m + 1]).then_inc(hi_ready, 1)

            def even_quad(b, pair):
                n = 2 * b + pair
                wait(act, pv_done, 16 * b + 8 * pair + 4)
                wait(act, odd_out, 2 * n)
                act.activation(even_ctx[:, :], pv_bank[0][:, :], ACT.Copy,
                               scale=half_lo[:, 0:1]).then_inc(even_out, 1)
                act.activation(even_sum[:, :], pv_bank[0][:, :], ACT.Copy,
                               scale=half_hi[:, 0:1]).then_inc(even_out, 1)

            def b2_copy(b):
                wait(act, b2_done, b + 1)
                wait(act, yb_ready, b)
                act.activation(b2_all[:, :], misc[0][:, 0:D], ACT.Copy).then_inc(b2_ready, 1)

            def w21_copy(b):
                wait(act, w21_done, b + 1)
                wait(act, z_done, 2 * b)
                act.activation(w21[:, :, :], misc[0][:, :].rearrange("p (f d) -> p f d", f=F),
                               ACT.Copy).then_inc(w21_ready, 1)

            def turn(b, post, prep, load):
                for u in range(UNITS):
                    exp(b, u)
                    if prep:
                        if u == 12:
                            xT_copy(b + 1, 0, 1)
                        if u == 13:
                            xT_copy(b + 1, 1, 0)
                        if u in (20, 22, 24, 26):
                            i = (u - 20) // 2
                            hi_half(b + 1, i, 1 - i % 2)
                    if u in (20, 52):
                        even_quad(b, u // 32)
                    if post:
                        if u == 29:
                            b2_copy(b - 1)
                        if u in (31, 32):
                            f = u - 31
                            yT_copy(b - 1, f, 1 - f, prep)
                    if u == 60:
                        w21_copy(b)

            act.wait_ge(const_in, CONSTS)
            act.activation(wq[:, :, :], wq_in[:, :, :], ACT.Copy, scale=SCALE).then_inc(act_set, 1)
            act.activation(bqk[:, 0, :], bq_in[:, :], ACT.Copy, scale=SCALE).then_inc(act_set, 1)
            xT_copy(0, 0, 1)
            xT_copy(0, 1, 0)
            act.wait_ge(act_set, 2)
            act.wait_ge(dve_set, 8)
            for i in range(4):
                hi_half(0, i, 1 - i % 2)
            turns(act, turn)
            b2_copy(LAST)
            yT_copy(LAST, 0, 1, False)
            yT_copy(LAST, 1, 0, False)

        @block.vector
        def _(dve):
            def row_max(b, n):
                g = n // 16
                wait(dve, nat_done, UNITS * b + n + 1)
                if n % 16 == 0:
                    wait(dve, maxT_done, 4 * b + g - 1)
                dve.tensor_reduce(neg_max[:, g % 2, n % 16:n % 16 + 1], nat_bank[n % 2][:, :], AX.X, ALU.max,
                                  negate=True).then_inc(max_done, 1)

            def max_halves(b, g, bank):
                wait(dve, maxT_done, 4 * b + g + 1)
                wait(dve, max_rows, 32 * (4 * b + g))
                dve.tensor_copy(max_hi[:, :], misc[bank][0:16, 0:P]).then_inc(maxhi_ready, 1)
                wait(dve, maxhi_ready, 4 * b + g + 1)
                dve.tensor_tensor(max_lo[:, :], misc[bank][0:16, 0:P], max_hi[:, :].bitcast(F32),
                                  ALU.subtract).then_inc(max_ready, 1)

            def statistics(which, b, src, c0, c1):
                wait(dve, aggr_done[which], 4 * b)
                for c in range(c0, c1):
                    dve.bn_stats(stats[which][:, c, :], src[:, c, :]).then_inc(stat_done[which], 1)

            def aggregate(which, b):
                wait(dve, stat_done[which], 4 * b + 4)
                wait_apart(dve, norm_ready[which], 4 * b)
                for c in range(C):
                    dve.bn_aggr(mean_var[which][:, c, :], stats[which][:, c, :]).then_inc(aggr_done[which], 1)

            def normalise(which, b, src, c0, c1):
                wait(dve, rstd_ready[which], b + 1)
                for c in range(c0, c1):
                    dve.tensor_scalar(normed[:, c, :], src[:, c, :], mean_var[which][:, c, 0:1],
                                      rstd[which][:, c:c + 1], ALU.subtract,
                                      ALU.mult).then_inc(norm_ready[which], 1)

            def lo_half(b, i, bank):
                which, m = i % 2, i // 2
                wait(dve, hi_ready, 4 * b + i + 1)
                dve.scalar_tensor_tensor(lo[:, which, m, :], misc[bank][:, :], bqk[:, which, m:m + 1],
                                         hi[:, which, m, :].bitcast(F32), ALU.add,
                                         ALU.subtract).then_inc(lo_ready, 1)

            def v_copy(b, half, bank):
                wait(dve, v_done, 2 * b + half + 1)
                wait(dve, v_stacked, 4 * b)
                dve.tensor_tensor(v_nat[:, 2 * half:2 * half + 2, :],
                                  misc[bank][:, :].rearrange("p (c d) -> p c d", c=2), bv_all[:, :, :],
                                  ALU.add).then_inc(v_ready, 1)

            def odd_quad(b, pair):
                n = 2 * b + pair
                wait(dve, pv_done, 16 * b + 8 * pair + 8)
                wait(dve, even_out, 2 * n + 2)
                wait(dve, attn_ready, n)
                dve.scalar_tensor_tensor(pair_ctx[:, :], pv_bank[1][:, :], half_hi[:, 0:1], even_ctx[:, :],
                                         ALU.mult, ALU.add).then_inc(odd_out, 1)
                dve.scalar_tensor_tensor(pair_sum[:, :], pv_bank[1][:, :], half_lo[:, 0:1], even_sum[:, :],
                                         ALU.mult, ALU.add).then_inc(odd_out, 1)
                wait_apart(dve, odd_out, 2 * n + 2)
                dve.stream_shuffle(sum_here[:, :], pair_sum[:, :],
                                   [(i + 16) % 32 for i in range(32)]).then_inc(sum_ready, 1)

            def invert(b, pair, c):
                n = 2 * b + pair
                if c == 0:
                    wait_apart(dve, sum_ready, n + 1)
                dve.reciprocal(inv_sum[:, c * P:(c + 1) * P], sum_here[:, c * P:(c + 1) * P]).then_inc(inv_ready, 1)

            def y_half(b, half, bank):
                wait(dve, wo_done, 2 * b + half + 1)
                wait(dve, xbo_ready, b + 1)
                wait(dve, yb_ready, b)
                wait(dve, norm_ready[1], 4 * b)
                dve.tensor_tensor(y[:, 2 * half:2 * half + 2, :],
                                  misc[bank][:, :].rearrange("p (c d) -> p c d", c=2),
                                  x_bo[:, 2 * half:2 * half + 2, :], ALU.add).then_inc(y_ready, 1)
                wait(dve, y_ready, 2 * b + half + 1)
                statistics(1, b, y, 2 * half, 2 * half + 2)

            def out_half(b, half, bank):
                wait(dve, z_done, 2 * b + half + 1)
                wait(dve, yb_ready, b + 1)
                wait(dve, stored, 32 * b)
                dve.tensor_tensor(res[:, 2 * half:2 * half + 2, :],
                                  misc[bank][:, :].rearrange("p (c d) -> p c d", c=2),
                                  y_b[:, 2 * half:2 * half + 2, :], ALU.add).then_inc(out_ready, 1)

            def turn(b, post, prep, load):
                for u in range(UNITS):
                    n = u + LEAD
                    if n < UNITS:
                        row_max(b, n)
                    elif prep:
                        row_max(b + 1, n - UNITS)
                    if prep:
                        if u in (0, 1):
                            if u == 0:
                                wait(dve, x_loaded, 16 * (b + 2))
                            statistics(0, b + 1, x_in, 2 * u, 2 * u + 2)
                        if u == 2:
                            aggregate(0, b + 1)
                    if post and u == 4:
                        odd_quad(b - 1, 1)
                    if post and 5 <= u < 9:
                        invert(b - 1, 1, u - 5)
                    if prep:
                        if u == 7:
                            wait(dve, xT_done, 2 * (b + 1))
                            wait(dve, yT_done, 2 * (b - 1) if post else 0)
                        if u in (7, 8):
                            normalise(0, b + 1, x_in, 2 * (u - 7), 2 * (u - 7) + 2)
                        if u in (9, 10):
                            v_copy(b + 1, u - 9, u - 9)
                    if u == 11:
                        max_halves(b, 1, 0)
                    if post:
                        if u in (16, 18):
                            half = (u - 16) // 2
                            y_half(b - 1, half, 1 - half)
                        if u == 19:
                            aggregate(1, b - 1)
                    if prep and u in (20, 22, 24, 26):
                        i = (u - 20) // 2
                        lo_half(b + 1, i, 1 - i % 2)
                    if post:
                        if u == 25:
                            wait(dve, xT_done, 2 * (b + 2) if prep else 0)
                            wait(dve, yT_done, 2 * (b - 1))
                        if u in (25, 26):
                            normalise(1, b - 1, y, 2 * (u - 25), 2 * (u - 25) + 2)
                    if u == 27:
                        max_halves(b, 2, 1)
                    if post and u in (35, 37):
                        half = (u - 35) // 2
                        out_half(b - 1, half, 1 - half)
                    if u == 36:
                        odd_quad(b, 0)
                    if 37 <= u < 41:
                        invert(b, 0, u - 37)
                    if u == 43:
                        max_halves(b, 3, 1)
                    if u == 60 and prep:
                        max_halves(b + 1, 0, 1)

            dve.memset(ones[:, :], 1.0).then_inc(dve_set, 1)
            dve.wait_ge(pool_set, 3)
            halves = ident[:, :].rearrange("p (j h d) -> p h j d", j=4, h=2)
            dve.tensor_reduce(half_lo[:, :], halves[:, 0], AX.XY, ALU.add).then_inc(dve_set, 1)
            dve.tensor_reduce(half_hi[:, :], halves[:, 1], AX.XY, ALU.add).then_inc(dve_set, 1)
            dve.wait_ge(x_loaded, 16)
            statistics(0, 0, x_in, 0, 4)
            aggregate(0, 0)
            normalise(0, 0, x_in, 0, 4)
            dve.memset(qs[ZROW:MROW, :, :].bitcast(F32), 0.0).then_inc(dve_set, 1)
            dve.memset(ks[ZROW:MROW, :, :].bitcast(F32), 0.0).then_inc(dve_set, 1)
            dve.memset(ks[MROW:KS, :, :].bitcast(F32), 1.0).then_inc(dve_set, 1)
            dve.memset(vs[:, :, :, :], 1.0).then_inc(dve_set, 1)
            dve.memset(b2_all[:, :], 0.0).then_inc(dve_set, 1)
            dve.wait_ge(act_set, 2)
            dve.wait_ge(const_in, CONSTS)
            for i in range(4):
                lo_half(0, i, 1 - i % 2)
            v_copy(0, 0, 0)
            v_copy(0, 1, 1)
            for n in range(LEAD):
                row_max(0, n)
                if n == 19:
                    max_halves(0, 0, 1)
            turns(dve, turn)
            odd_quad(LAST, 1)
            for c in range(C):
                invert(LAST, 1, c)
            y_half(LAST, 0, 1)
            y_half(LAST, 1, 0)
            aggregate(1, LAST)
            dve.wait_ge(yT_done, 2 * LAST)
            normalise(1, LAST, y, 0, 4)
            out_half(LAST, 0, 1)
            out_half(LAST, 1, 0)

        @block.gpsimd
        def _(pool):
            def inverse_root(which, b):
                wait(pool, aggr_done[which], 4 * b + 4)
                wait_apart(pool, norm_ready[which], 4 * b)
                pool.tensor_scalar(var_eps[which][:, :], mean_var[which][:, :, 1], EPS, None,
                                   ALU.add).then_inc(eps_done[which], 1)
                wait(pool, eps_done[which], b + 1)
                pool.tensor_tensor(rstd[which][:, :], var_eps[which][:, :], neg_half[:, :],
                                   ALU.pow).then_inc(rstd_ready[which], 1)

            def v_stack(b, g):
                wait(pool, v_ready, 2 * b + 2)
                wait_apart(pool, pv_done, 16 * (b - 1) + 4 * g + 4)
                at = 16 * (g % 2)
                pool.tensor_copy(vs[:, :, 4 * g:4 * g + 4, at:at + 16],
                                 v_nat[:, :, 64 * g:64 * g + 64].rearrange("p c (h d) -> p c h d", h=4))\
                    .then_inc(v_stacked, 1)

            def divide(b, pair):
                n = 2 * b + pair
                wait(pool, inv_ready, 4 * n + 4)
                wait(pool, wo_done, 2 * b)
                pool.tensor_tensor(attnT[:, pair, :], pair_ctx[:, :], inv_sum[:, :],
                                   ALU.mult).then_inc(attn_ready, 1)

            def keep_next(b):
                wait(pool, x_loaded, 16 * (b + 1))
                wait(pool, xbo_ready, b)
                for c in range(C):
                    last = pool.tensor_tensor(x_bo_next[:, c, :], x_in[:, c, :], bo_all[:, :], ALU.add)
                last.then_inc(xbo_next_ready, 1)

            def keep(b):
                wait(pool, xbo_next_ready, b + 1)
                wait_apart(pool, y_ready, 2 * b)
                pool.tensor_copy(x_bo[:, :, :], x_bo_next[:, :, :]).then_inc(xbo_ready, 1)

            def add_b2(b):
                wait(pool, y_ready, 2 * b + 2)
                wait(pool, b2_ready, b + 1)
                wait(pool, out_ready, 2 * b)
                for c in range(C):
                    last = pool.tensor_tensor(y_b[:, c, :], y[:, c, :], b2_all[:, :], ALU.add)
                last.then_inc(yb_ready, 1)

            def b2_parts(b):
                wait(pool, ffn_loaded, 64 * (b + 1))
                wait(pool, b2_done, b)
                pool.tensor_tensor(b2_part[:, :, :], w2_in[:, :, :], b1_in[:, :].unsqueeze(2).to_broadcast([P, OC, D]),
                                   ALU.mult).then_inc(b2_step, 1)
                for k, width in enumerate((4, 2, 1)):
                    wait(pool, b2_step, 4 * b + k + 1)
                    pool.tensor_tensor(b2_part[:, 0:width, :], b2_part[:, 0:width, :],
                                       b2_part[:, width:2 * width, :], ALU.add).then_inc(b2_step, 1)
                wait(pool, b2_step, 4 * b + 4)
                pool.tensor_tensor(b2_part[0:1, 0, :], b2_part[0:1, 0, :], b2_in[:, :],
                                   ALU.add).then_inc(b2_part_ready, 1)

            def turn(b, post, prep, load):
                if prep:
                    inverse_root(0, b + 1)
                if post:
                    v_stack(b, 3)
                    divide(b - 1, 1)
                    inverse_root(1, b - 1)
                keep(b)
                if prep:
                    keep_next(b + 1)
                    v_stack(b + 1, 0)
                if post:
                    add_b2(b - 1)
                if prep:
                    v_stack(b + 1, 1)
                divide(b, 0)
                b2_parts(b)
                if prep:
                    v_stack(b + 1, 2)

            pool.memset(ident[:, :], 0.0).then_inc(pool_set, 1)
            pool.memset(neg_half[:, :], -0.5).then_inc(pool_set, 1)
            pool.wait_ge(pool_set, 1)
            pool.affine_select(out=ident[:, :], in_=ident[:, :], compare_op=ALU.not_equal, fill=1.0, base=0,
                               pattern=[[-1, P]], channel_multiplier=1).then_inc(pool_set, 1)
            pool.wait_ge(pool_set, 3)
            inverse_root(0, 0)
            pool.wait_ge(const_in, CONSTS)
            pool.wait_ge(dve_set, 8)
            keep_next(0)
            for g in range(QUADS):
                v_stack(0, g)
            turns(pool, turn)
            divide(LAST, 1)
            inverse_root(1, LAST)
            add_b2(LAST)


def kernel(**inputs):
    import numpy as np
    import concourse.bacc as bacc
    from concourse.bass_utils import run_bass_kernel_spmd

    a = {k: np.asarray(v) for k, v in inputs.items()}
    def by_quad(w):
        return w.reshape((2, 2, 4, HD) + w.shape[1:]).swapaxes(2, 3).reshape(w.shape)

    wo_rows = a["L0_xattn_Wo"].T.reshape(2, 2, 4, HD, D).transpose(0, 2, 1, 3, 4).reshape(D, D)
    arrays = {
        "x": a["x"],
        "ctxT": a["ctx_1024"].transpose(0, 2, 1).reshape(B, F, P, S),
        "wqT": by_quad(a["L0_xattn_Wq"]).T,
        "bq": by_quad(a["L0_xattn_bq"]).reshape(2, P).T,
        "wkT": by_quad(a["L0_xattn_Wk"]).T,
        "bk": by_quad(a["L0_xattn_bk"]).reshape(2, P).T,
        "wvT": a["L0_xattn_Wv"].T,
        "bv": a["L0_xattn_bv"],
        "woT": wo_rows,
        "bo": a["L0_xattn_bo"],
        "w1": a["L0_ffn_W1"],
        "b1": a["L0_ffn_b1"],
        "w2T": a["L0_ffn_W2"].transpose(0, 2, 1),
        "b2": a["L0_ffn_b2"],
    }
    nc = bacc.Bacc("TRN2", target_bir_lowering=False, num_devices=1)
    arrays = {k: np.ascontiguousarray(v) for k, v in arrays.items()}
    args = [nc.dram_tensor(k, v.shape, mybir.dt.from_np(v.dtype), kind="ExternalInput").ap()
            for k, v in arrays.items()]
    args.append(nc.dram_tensor("out", (B, S, D), F32, kind="ExternalOutput").ap())
    xattn_ffn(nc, *args)
    r = run_bass_kernel_spmd(nc, [arrays], core_ids=[0])
    return r.results[0]["out"]
```

```python
from contextlib import ExitStack

import concourse.bass as bass
from concourse import mybir

F32 = mybir.dt.float32
F32R = mybir.dt.float32r
ALU = mybir.AluOpType
ACT = mybir.ActivationFunctionType
AX = mybir.AxisListType

P = 128
B = 8
S = 512
D = 256
H = 16
HD = D // H
INTER = 1024
C = S // P
F = D // P
OC = INTER // P
QUADS = H // 4
UNITS = QUADS * 16
LEAD = 28
EPS = 1e-5
SCALE = float(HD) ** -0.5
SLOTS = ((0, 0), (1, 0), (0, 1), (1, 1))
ZROW, MROW = 64, 96
KN, KS = MROW, MROW + 2
NATS = 3
LAST = B - 1


def xattn_ffn(nc, x, ctxT, wqT, bq, wkT, bk, wvT, bv, woT, bo, w1, b1, w2T, b2, out):
    with ExitStack() as stack:
        def sb(name, shape, dt=F32):
            return stack.enter_context(nc.sbuf_tensor(name, shape, dt))

        def pb(name):
            return stack.enter_context(nc.psum_tensor(name, [P, S], F32))

        def sem(name):
            return stack.enter_context(nc.semaphore(name))

        ident = sb("ident", [P, P])
        ones = sb("ones", [P, P])
        half_lo = sb("half_lo", [P, 1])
        half_hi = sb("half_hi", [P, 1])
        neg_half = sb("neg_half", [P, C])
        wq_in = sb("wq_in", [P, F, D])
        wq = sb("wq", [P, F, D])
        wk = sb("wk", [P, F, D])
        wv = sb("wv", [P, F, D])
        wo = sb("wo", [P, F, D])
        bq_in = sb("bq_in", [P, 2])
        bqk = sb("bqk", [P, 2, 2])
        bv_all = sb("bv_all", [P, 2, D])
        bo_all = sb("bo_all", [P, D])
        x_in = sb("x_in", [P, C, D])
        x_bo_next = sb("x_bo_next", [P, C, D])
        x_bo = sb("x_bo", [P, C, D])
        ctx_in = sb("ctx_in", [P, F, S])
        normed = sb("normed", [P, C, D])
        normedT = sb("normedT", [P, F, S])
        stats = [sb(f"stats{i}", [P, C, 6]) for i in range(2)]
        mean_var = [sb(f"mean_var{i}", [P, C, 2]) for i in range(2)]
        var_eps = [sb(f"var_eps{i}", [P, C]) for i in range(2)]
        rstd = [sb(f"rstd{i}", [P, C]) for i in range(2)]
        shift = [sb(f"shift{i}", [P, C]) for i in range(2)]
        hi = sb("hi", [P, 2, 2, S], F32R)
        lo = sb("lo", [P, 2, 2, S], F32R)
        qs = sb("qs", [P, H, S], F32R)
        ks = sb("ks", [P, H, S], F32R)
        v_nat = sb("v_nat", [P, C, D])
        vs = sb("vs", [P, C, H, 32])
        neg_max = sb("neg_max", [P, 2, 16])
        max_hi = sb("max_hi", [16, P], F32R)
        max_lo = sb("max_lo", [16, P], F32R)
        probs = [sb(f"probs{i}", [P, 4, S]) for i in range(2)]
        even_ctx = sb("even_ctx", [P, S])
        even_sum = sb("even_sum", [P, S])
        pair_ctx = sb("pair_ctx", [P, S])
        odd_sum = sb("odd_sum", [P, S])
        sums = sb("sums", [P, 32])
        inv_small = sb("inv_small", [P, 32])
        inv_sum = sb("inv_sum", [P, S])
        attnT = sb("attnT", [P, 2, S])
        y = sb("y", [P, C, D])
        y_b = sb("y_b", [P, C, D])
        res = sb("res", [P, C, D])
        w1_in = sb("w1_in", [P, OC, D])
        w2_in = sb("w2_in", [P, OC, D])
        b1_in = sb("b1_in", [P, OC])
        b2_in = sb("b2_in", [1, D])
        b2_part = sb("b2_part", [P, OC, D])
        b2_all = sb("b2_all", [P, D])
        w21 = sb("w21", [P, F, D])

        inv_dram = nc.dram_tensor("inv_dram", (4, 2, S), F32, kind="Internal").ap()

        st_bank = [pb("st0"), pb("st1")]
        nat_bank = [pb(f"nat{i}") for i in range(NATS)]
        pv_bank = pb("pv")
        misc = [pb("misc0"), pb("misc1")]

        const_qk = sem("const_qk")
        const_in = sem("const_in")
        x_loaded = sem("x_loaded")
        ctx_loaded = sem("ctx_loaded")
        ffn_loaded = sem("ffn_loaded")
        stacked = [sem(f"stacked{g}") for g in range(QUADS)]
        max_rows = sem("max_rows")
        sums_in = sem("sums_in")
        inv_saved = sem("inv_saved")
        inv_ready = sem("inv_ready")
        stored = sem("stored")
        pool_set = sem("pool_set")
        rows_set = sem("rows_set")
        dve_set = sem("dve_set")
        act_set = sem("act_set")
        st_done = sem("st_done")
        nat_done = sem("nat_done")
        pv_done = sem("pv_done")
        maxT_done = sem("maxT_done")
        xT_done = sem("xT_done")
        qk_done = sem("qk_done")
        v_done = sem("v_done")
        wo_done = sem("wo_done")
        b2_done = sem("b2_done")
        yT_done = sem("yT_done")
        z_done = sem("z_done")
        w21_done = sem("w21_done")
        exp_done = sem("exp_done")
        xT_ready = sem("xT_ready")
        yT_ready = sem("yT_ready")
        hi_ready = sem("hi_ready")
        even_out = sem("even_out")
        odd_copied = sem("odd_copied")
        b2_ready = sem("b2_ready")
        w21_ready = sem("w21_ready")
        max_done = sem("max_done")
        lo_ready = sem("lo_ready")
        maxhi_ready = sem("maxhi_ready")
        max_ready = sem("max_ready")
        v_ready = sem("v_ready")
        odd_out = sem("odd_out")
        recip_ready = sem("recip_ready")
        y_ready = sem("y_ready")
        out_ready = sem("out_ready")
        stat_done = [sem("xstat_done"), sem("ystat_done")]
        aggr_done = [sem("xaggr_done"), sem("yaggr_done")]
        root_step = [sem("xroot_step"), sem("yroot_step")]
        rstd_ready = [sem("xrstd_ready"), sem("yrstd_ready")]
        norm_ready = [sem("xnorm_ready"), sem("ynorm_ready")]
        v_stacked = sem("v_stacked")
        attn_ready = sem("attn_ready")
        xbo_next_ready = sem("xbo_next_ready")
        xbo_ready = sem("xbo_ready")
        yb_ready = sem("yb_ready")
        b2_step = sem("b2_step")
        b2_part_ready = sem("b2_part_ready")

        passed = {e.engine: sem(f"passed_{n}") for e, n in
                  ((nc.sync, "sp"), (nc.vector, "dve"), (nc.gpsimd, "pool"))}

        CONSTS_QK = 4 * 16
        CONSTS = 5 * 16

        def wait(eng, s, value):
            if not (isinstance(value, int) and value <= 0):
                eng.wait_ge(s, value)

        def wait_apart(eng, s, value):
            wait(eng, s, value)
            if not isinstance(value, int):
                eng.sem_inc(passed[eng.engine], 1)

        def turns(eng, turn):
            turn(0, False, True, True)
            turn(1, True, True, True)
            with eng.Fori(2, B - 2) as b:
                turn(b, True, True, True)
            turn(B - 2, True, True, False)
            turn(B - 1, True, False, False)

        block = stack.enter_context(nc.Block())

        @block.sync
        def _(sp):
            def load_x(b):
                sp.dma_start(x_in[:, :, :], x[b].rearrange("(p c) d -> p c d", c=C)).then_inc(x_loaded, 16)

            def load_ctx(b):
                sp.dma_start(ctx_in[:, :, :], ctxT[b].rearrange("f p s -> p f s")).then_inc(ctx_loaded, 16)

            def load_ffn(b):
                sp.dma_start(w1_in[:, :, :], w1[b].rearrange("(p o) d -> p o d", o=OC)).then_inc(ffn_loaded, 16)
                sp.dma_start(w2_in[:, :, :], w2T[b].rearrange("(p o) d -> p o d", o=OC)).then_inc(ffn_loaded, 16)
                sp.dma_start(b1_in[:, :], b1[b].rearrange("(p o) -> p o", o=OC)).then_inc(ffn_loaded, 16)
                sp.dma_start(b2_in[:, :], b2[b].rearrange("(a d) -> a d", a=1)).then_inc(ffn_loaded, 16)

            def stack_quad(b, g):
                wait_apart(sp, lo_ready, 4 * b + 2 * (g // 2) + 2)
                wait_apart(sp, st_done, UNITS * (b - 1) + 16 * g + 16)
                rows = slice(64 * (g % 2), 64 * (g % 2) + 64)
                for s, halves in enumerate(SLOTS):
                    for which, dst in ((0, qs), (1, ks)):
                        src = (hi, lo)[halves[which]]
                        sp.dma_start(dst[16 * s:16 * s + 16, 4 * g:4 * g + 4, :].bitcast(F32),
                                     src[rows, which, g // 2, :].bitcast(F32)).then_inc(stacked[g], 16)

            def store_max(b, g):
                wait_apart(sp, max_ready, 4 * b + g + 1)
                wait_apart(sp, st_done, UNITS * (b - 1) + 16 * g + 16)
                for r, src in enumerate((max_hi, max_lo)):
                    dst = qs[MROW + r:MROW + r + 1, 4 * g:4 * g + 4, :].bitcast(F32)
                    sp.dma_start(dst.rearrange("a h (c t) -> a (h c) t", c=C),
                                 src[:, :].bitcast(F32)).then_inc(max_rows, 16)

            def store_out(b, half):
                wait_apart(sp, out_ready, 2 * b + half + 1)
                sp.dma_start(out[b].rearrange("(p c) d -> p c d", c=C)[:, 2 * half:2 * half + 2, :],
                             res[:, 2 * half:2 * half + 2, :]).then_inc(stored, 16)

            def gather_sums(b, pair):
                n = 2 * b + pair
                wait_apart(sp, even_out, 2 * n + 2)
                wait_apart(sp, odd_copied, n + 1)
                wait_apart(sp, recip_ready, n)
                sp.dma_start(sums[0:64, :], even_sum[16:P:32, :]).then_inc(sums_in, 16)
                sp.dma_start(sums[64:P, :], odd_sum[0:P:32, :]).then_inc(sums_in, 16)

            def save_inverse(b, pair):
                n = 2 * b + pair
                wait_apart(sp, recip_ready, n + 1)
                wait_apart(sp, inv_ready, 16 * n)
                for t in range(2):
                    sp.dma_start(inv_dram[:, t, :].rearrange("j (k i) -> j k i", i=32),
                                 inv_small[64 * t:64 * t + 64, :]).then_inc(inv_saved, 16)

            def spread_inverse(b, pair):
                n = 2 * b + pair
                wait_apart(sp, inv_saved, 32 * n + 32)
                wait_apart(sp, attn_ready, n)
                sp.dma_start(inv_sum[:, :],
                             inv_dram.rearrange("j t s -> (j t) s").unsqueeze(1).to_broadcast([8, HD, S]))\
                    .then_inc(inv_ready, 16)

            def turn(b, post, prep, load):
                if post:
                    gather_sums(b - 1, 1)
                    stack_quad(b, 3)
                store_max(b, 1)
                if post:
                    save_inverse(b - 1, 1)
                    wait_apart(sp, w21_done, b)
                    wait_apart(sp, b2_part_ready, b)
                    load_ffn(b)
                    spread_inverse(b - 1, 1)
                if prep:
                    stack_quad(b + 1, 0)
                store_max(b, 2)
                if prep:
                    stack_quad(b + 1, 1)
                gather_sums(b, 0)
                store_max(b, 3)
                if post:
                    store_out(b - 1, 0)
                    store_out(b - 1, 1)
                save_inverse(b, 0)
                if load:
                    wait_apart(sp, norm_ready[0], 4 * (b + 2))
                    wait_apart(sp, xbo_next_ready, b + 2)
                    load_x(b + 2)
                spread_inverse(b, 0)
                if load:
                    wait_apart(sp, v_done, 2 * (b + 2))
                    wait_apart(sp, qk_done, 4 * (b + 2))
                    load_ctx(b + 2)
                if prep:
                    stack_quad(b + 1, 2)
                    store_max(b + 1, 0)

            load_x(0)
            load_ctx(0)
            sp.dma_start(wq_in[:, :, :], wqT.rearrange("(f p) d -> p f d", p=P)).then_inc(const_qk, 16)
            sp.dma_start(bq_in[:, :], bq).then_inc(const_qk, 16)
            sp.dma_start(wk[:, :, :], wkT.rearrange("(f p) d -> p f d", p=P)).then_inc(const_qk, 16)
            sp.dma_start(bqk[:, 1, :], bk).then_inc(const_qk, 16)
            sp.dma_start(wv[:, :, :], wvT.rearrange("(f p) d -> p f d", p=P)).then_inc(const_in, 16)
            for i in range(2):
                sp.dma_start(bv_all[:, i, :], bv.partition_broadcast(P)).then_inc(const_in, 16)
            sp.dma_start(bo_all[:, :], bo.partition_broadcast(P)).then_inc(const_in, 16)
            sp.dma_start(wo[:, :, :], woT.rearrange("(f p) d -> p f d", p=P)).then_inc(const_in, 16)
            for g in range(QUADS):
                stack_quad(0, g)
            sp.wait_ge(norm_ready[0], 4)
            sp.wait_ge(xbo_next_ready, 1)
            load_x(1)
            sp.wait_ge(v_done, 2)
            sp.wait_ge(qk_done, 4)
            load_ctx(1)
            store_max(0, 0)
            load_ffn(0)
            turns(sp, turn)
            gather_sums(LAST, 1)
            save_inverse(LAST, 1)
            spread_inverse(LAST, 1)
            store_out(LAST, 0)
            store_out(LAST, 1)
            sp.wait_ge(stored, 32 * B)

        @block.tensor
        def _(pe):
            mm = nc.tensor.matmul

            def nat(b, n):
                g, j, c = n // 16, n % 16 // 4, n % 4
                h = 4 * g + j
                if n % 16 == 0:
                    wait(pe, stacked[g], 128 * (b + 1))
                wait(pe, max_done, UNITS * b + (0, -2, -1)[n] if n < NATS else UNITS * b + n - 2)
                mm(nat_bank[n % NATS][:, :], qs[0:KN, h, c * P:(c + 1) * P], ks[0:KN, h, :],
                   start=True, stop=True).then_inc(nat_done, 1)

            def st(b, u):
                g, kc, j = u // 16, u % 16 // 4, u % 4
                h = 4 * g + j
                if u % 16 == 0:
                    wait(pe, max_rows, 32 * (4 * b + g + 1))
                wait(pe, exp_done, UNITS * b + u - 1)
                mm(st_bank[u % 2][:, :], ks[0:KS, h, kc * P:(kc + 1) * P], qs[0:KS, h, :],
                   start=True, stop=True).then_inc(st_done, 1)

            def pv(b, n):
                g, kc = n // 4, n % 4
                if kc == 0:
                    wait(pe, v_stacked, 4 * b + g + 1)
                    pair = 2 * b + g // 2
                    if g % 2:
                        wait(pe, even_out, 2 * pair + 2)
                    else:
                        wait(pe, odd_out, pair)
                wait(pe, exp_done, UNITS * b + 4 * n + 4)
                for j in range(4):
                    last = mm(pv_bank[32 * j:32 * j + 32, :], vs[:, kc, 4 * g + j, :],
                              probs[n % 2][:, j, :], start=(kc == 0), stop=(kc == 3),
                              tile_position=(0, 32 * j), skip_group_check=True)
                last.then_inc(pv_done, 1)

            def transposeT(bank, f, done):
                for c in range(C):
                    last = nc.tensor.transpose(misc[bank][:, c * P:(c + 1) * P],
                                               normed[:, c, f * P:(f + 1) * P], ident[:, :])
                last.then_inc(done, 1)

            def xT(b, f, bank):
                wait(pe, norm_ready[0], 4 * b + 4)
                transposeT(bank, f, xT_done)

            def yT(b, f, bank):
                wait(pe, norm_ready[1], 4 * b + 4)
                transposeT(bank, f, yT_done)

            def maxT(b, g, bank):
                wait(pe, max_done, UNITS * b + 16 * g + 16)
                nc.tensor.transpose(misc[bank][0:16, 0:P], neg_max[:, g % 2, :],
                                    ident[:, :]).then_inc(maxT_done, 1)

            def qk(b, i, bank, f):
                which, m = i % 2, i // 2
                if which == 0:
                    wait(pe, xT_ready, 2 * b + 2)
                src, w = (normedT, wq) if which == 0 else (ctx_in, wk)
                last = mm(misc[bank][:, :], w[:, f, m * P:(m + 1) * P], src[:, f, :],
                          start=(f == 0), stop=(f == F - 1))
                if f == F - 1:
                    last.then_inc(qk_done, 1)

            def v(b, c, bank):
                if c == 0:
                    wait(pe, ctx_loaded, 16 * (b + 1))
                for f in range(F):
                    last = mm(misc[bank][:, (c % 2) * D:(c % 2 + 1) * D], ctx_in[:, f, c * P:(c + 1) * P],
                              wv[:, f, :], start=(f == 0), stop=(f == F - 1))
                if c % 2:
                    last.then_inc(v_done, 1)

            def wo_(b, c, bank):
                if c == 0:
                    wait(pe, attn_ready, 2 * b + 2)
                for f in range(F):
                    last = mm(misc[bank][:, (c % 2) * D:(c % 2 + 1) * D], attnT[:, f, c * P:(c + 1) * P],
                              wo[:, f, :], start=(f == 0), stop=(f == F - 1))
                if c % 2:
                    last.then_inc(wo_done, 1)

            def b2sum(b, bank):
                wait(pe, b2_part_ready, b + 1)
                mm(misc[bank][:, 0:D], ones[:, :], b2_part[:, 0, :], start=True, stop=True).then_inc(b2_done, 1)

            def z(b, c, bank):
                if c == 0:
                    wait(pe, yT_ready, 2 * b + 2)
                    wait(pe, w21_ready, b + 1)
                for f in range(F):
                    last = mm(misc[bank][:, (c % 2) * D:(c % 2 + 1) * D], normedT[:, f, c * P:(c + 1) * P],
                              w21[:, f, :], start=(f == 0), stop=(f == F - 1))
                if c % 2:
                    last.then_inc(z_done, 1)

            def w21_part(b, n, bank):
                f, o = n // OC, n % OC
                if n == 0:
                    wait(pe, ffn_loaded, 64 * (b + 1))
                last = mm(misc[bank][:, f * D:(f + 1) * D], w1_in[:, o, f * P:(f + 1) * P], w2_in[:, o, :],
                          start=(o == 0), stop=(o == OC - 1))
                if n == F * OC - 1:
                    last.then_inc(w21_done, 1)

            def jobs(b, u, post, prep):
                if prep:
                    if u == 4:
                        wait(pe, w21_ready, b)
                        wait(pe, v_ready, 2 * b + 2)
                    if u in (4, 5):
                        v(b + 1, u - 4, 0)
                if u == 6:
                    wait(pe, max_ready, 4 * b + 1)
                    maxT(b, 1, 1)
                if prep:
                    if u == 8:
                        wait(pe, v_ready, 2 * b + 3)
                    if u in (8, 9):
                        v(b + 1, u - 6, 0)
                    if u == 10:
                        wait(pe, max_ready, 4 * b + 2)
                        xT(b + 1, 0, 1)
                    if u == 12:
                        wait(pe, v_ready, 2 * b + 4)
                        xT(b + 1, 1, 0)
                    if 13 <= u < 21:
                        i, f = (u - 13) // 2, (u - 13) % 2
                        if i >= 2 and f == 0:
                            wait(pe, lo_ready, 4 * b + i + 3)
                        qk(b + 1, i, 1 - i % 2, f)
                if u == 22:
                    wait(pe, lo_ready, 4 * b + 7 if prep else 0)
                    wait(pe, max_ready, 4 * b + 2)
                    maxT(b, 2, 1)
                if post:
                    if u == 23:
                        wait(pe, lo_ready, 4 * b + 8 if prep else 0)
                        wait(pe, w21_ready, b)
                    if u in (23, 24):
                        wo_(b - 1, u - 23, 0)
                    if u == 25:
                        wait(pe, max_ready, 4 * b + 3)
                    if u in (25, 26):
                        wo_(b - 1, u - 23, 1)
                    if u == 28:
                        wait(pe, y_ready, 2 * b - 1)
                        b2sum(b - 1, 0)
                    if u == 34:
                        wait(pe, y_ready, 2 * b)
                        yT(b - 1, 0, 1)
                    if u == 35:
                        wait(pe, b2_ready, b)
                        yT(b - 1, 1, 0)
                if u == 37:
                    wait(pe, yT_ready, 2 * b - 1 if post else 0)
                    wait(pe, max_ready, 4 * b + 3)
                    maxT(b, 3, 1)
                if post:
                    if 38 <= u < 42:
                        c = u - 38
                        if c == 2:
                            wait(pe, max_ready, 4 * b + 4)
                        z(b - 1, c, c // 2)
                if u == 43:
                    wait(pe, out_ready, 2 * b - 1 if post else 0)
                    wait(pe, lo_ready, 4 * b + 8 if prep else 0)
                if 43 <= u < 59:
                    w21_part(b, u - 43, 0)
                if u == 54 and prep:
                    wait(pe, out_ready, 2 * b if post else 0)
                    wait(pe, max_ready, 4 * b + 4)
                    maxT(b + 1, 0, 1)

            def turn(b, post, prep, load):
                for u in range(UNITS):
                    st(b, u)
                    n = u + LEAD
                    if n < UNITS:
                        nat(b, n)
                    elif prep:
                        nat(b + 1, n - UNITS)
                    if u % 4 == 2:
                        if u > 4:
                            pv(b, u // 4 - 1)
                        elif post:
                            pv(b - 1, 15)
                    jobs(b, u, post, prep)

            pe.wait_ge(pool_set, 3)
            xT(0, 0, 1)
            xT(0, 1, 0)
            pe.wait_ge(act_set, 2)
            pe.wait_ge(const_qk, CONSTS_QK)
            pe.wait_ge(ctx_loaded, 16)
            for i, bank in enumerate((1, 0, 1, 0)):
                if i >= 2:
                    pe.wait_ge(lo_ready, i - 1)
                for f in range(F):
                    qk(0, i, bank, f)
            pe.wait_ge(const_in, CONSTS)
            for c in range(C):
                if c % 2 == 0:
                    pe.wait_ge(lo_ready, 4 if c == 0 else 3)
                v(0, c, c // 2)
            pe.wait_ge(rows_set, 4)
            pe.wait_ge(dve_set, 3)
            for n in range(LEAD):
                nat(0, n)
                if n == 18:
                    pe.wait_ge(v_ready, 2)
                    maxT(0, 0, 1)
            turns(pe, turn)
            pv(LAST, 15)
            pe.wait_ge(w21_ready, B)
            wo_(LAST, 0, 0)
            wo_(LAST, 1, 0)
            pe.wait_ge(out_ready, 2 * LAST)
            wo_(LAST, 2, 1)
            wo_(LAST, 3, 1)
            pe.wait_ge(y_ready, 2 * B)
            b2sum(LAST, 0)
            yT(LAST, 0, 1)
            pe.wait_ge(b2_ready, B)
            yT(LAST, 1, 0)
            for c in range(C):
                z(LAST, c, c // 2)

        @block.scalar
        def _(act):
            def exp(b, u):
                kc, j = u // 4, u % 4
                wait(act, st_done, UNITS * b + u + 1)
                if j == 0:
                    wait(act, pv_done, 16 * b + kc - 1)
                act.activation(probs[kc % 2][:, j, :], st_bank[u % 2][:, :], ACT.Exp).then_inc(exp_done, 1)

            def xT_copy(b, f, bank):
                wait(act, xT_done, 2 * b + f + 1)
                wait(act, z_done, 2 * (b - 2))
                wait(act, qk_done, 4 * (b - 1) + 3)
                act.activation(normedT[:, f, :], misc[bank][:, :], ACT.Copy).then_inc(xT_ready, 1)

            def yT_copy(b, f, bank, prep):
                wait(act, yT_done, 2 * b + f + 1)
                wait(act, qk_done, 4 * (b + 2) + 3 if prep else 0)
                wait(act, z_done, 2 * b)
                act.activation(normedT[:, f, :], misc[bank][:, :], ACT.Copy).then_inc(yT_ready, 1)

            def hi_half(b, i, bank):
                which, m = i % 2, i // 2
                wait(act, qk_done, 4 * b + i + 1)
                for g in (2 * m, 2 * m + 1):
                    wait(act, stacked[g], 128 * b)
                act.activation(hi[:, which, m, :], misc[bank][:, :], ACT.Identity,
                               bias=bqk[:, which, m:m + 1]).then_inc(hi_ready, 1)

            def even_quad(b, pair):
                n = 2 * b + pair
                wait(act, pv_done, 16 * b + 8 * pair + 4)
                wait(act, odd_out, n)
                wait(act, sums_in, 32 * n)
                act.activation(even_ctx[:, :], pv_bank[:, :], ACT.Copy,
                               scale=half_lo[:, 0:1]).then_inc(even_out, 1)
                act.activation(even_sum[:, :], pv_bank[:, :], ACT.Copy).then_inc(even_out, 1)

            def odd_quad(b, pair):
                n = 2 * b + pair
                wait(act, pv_done, 16 * b + 8 * pair + 8)
                wait(act, sums_in, 32 * n)
                act.activation(odd_sum[:, :], pv_bank[:, :], ACT.Copy).then_inc(odd_copied, 1)

            def normalise(which, b, src, c0, c1):
                wait(act, rstd_ready[which], b + 1)
                for c in range(c0, c1):
                    act.activation(normed[:, c, :], src[:, c, :], ACT.Identity, bias=shift[which][:, c:c + 1],
                                   scale=rstd[which][:, c:c + 1]).then_inc(norm_ready[which], 1)

            def b2_copy(b):
                wait(act, b2_done, b + 1)
                wait(act, yb_ready, b)
                act.activation(b2_all[:, :], misc[0][:, 0:D], ACT.Copy).then_inc(b2_ready, 1)

            def w21_copy(b):
                wait(act, w21_done, b + 1)
                wait(act, z_done, 2 * b)
                act.activation(w21[:, :, :], misc[0][:, :].rearrange("p (f d) -> p f d", f=F),
                               ACT.Copy).then_inc(w21_ready, 1)

            def turn(b, post, prep, load):
                for u in range(UNITS):
                    exp(b, u)
                    if post and u == 3:
                        odd_quad(b - 1, 1)
                    if prep:
                        if u == 6:
                            wait(act, xT_done, 2 * (b + 1))
                            wait(act, yT_done, 2 * (b - 1) if post else 0)
                        if u in (6, 7):
                            normalise(0, b + 1, x_in, 2 * (u - 6), 2 * (u - 6) + 2)
                        if u in (11, 13):
                            f = (u - 11) // 2
                            xT_copy(b + 1, f, 1 - f)
                        if u in (15, 17, 19, 21):
                            i = (u - 15) // 2
                            hi_half(b + 1, i, 1 - i % 2)
                    if u in (19, 51):
                        even_quad(b, u // 32)
                    if post:
                        if u == 29:
                            b2_copy(b - 1)
                        if u == 32:
                            wait(act, xT_done, 2 * (b + 2) if prep else 0)
                            wait(act, yT_done, 2 * (b - 1))
                        if u in (32, 33):
                            normalise(1, b - 1, y, 2 * (u - 32), 2 * (u - 32) + 2)
                        if u in (35, 36):
                            f = u - 35
                            yT_copy(b - 1, f, 1 - f, prep)
                    if u == 35:
                        odd_quad(b, 0)
                    if u == 59:
                        w21_copy(b)

            act.wait_ge(const_qk, CONSTS_QK)
            act.activation(wq[:, :, :], wq_in[:, :, :], ACT.Copy, scale=SCALE).then_inc(act_set, 1)
            act.activation(bqk[:, 0, :], bq_in[:, :], ACT.Copy, scale=SCALE).then_inc(act_set, 1)
            act.wait_ge(x_loaded, 16)
            normalise(0, 0, x_in, 0, C)
            xT_copy(0, 0, 1)
            xT_copy(0, 1, 0)
            act.wait_ge(act_set, 2)
            act.wait_ge(dve_set, 3)
            for i in range(4):
                hi_half(0, i, 1 - i % 2)
            turns(act, turn)
            odd_quad(LAST, 1)
            b2_copy(LAST)
            act.wait_ge(yT_done, 2 * LAST)
            normalise(1, LAST, y, 0, C)
            yT_copy(LAST, 0, 1, False)
            yT_copy(LAST, 1, 0, False)

        @block.vector
        def _(dve):
            def row_max(b, n):
                g = n // 16
                wait(dve, nat_done, UNITS * b + n + 1)
                if n % 16 == 0:
                    wait(dve, maxT_done, 4 * b + g - 1)
                dve.tensor_reduce(neg_max[:, g % 2, n % 16:n % 16 + 1], nat_bank[n % NATS][:, :], AX.X, ALU.max,
                                  negate=True).then_inc(max_done, 1)

            def max_halves(b, g, bank):
                wait(dve, maxT_done, 4 * b + g + 1)
                wait(dve, max_rows, 32 * (4 * b + g))
                dve.tensor_copy(max_hi[:, :], misc[bank][0:16, 0:P]).then_inc(maxhi_ready, 1)
                wait(dve, maxhi_ready, 4 * b + g + 1)
                dve.tensor_tensor(max_lo[:, :], misc[bank][0:16, 0:P], max_hi[:, :].bitcast(F32),
                                  ALU.subtract).then_inc(max_ready, 1)

            def statistics(which, b, src, c0, c1):
                wait(dve, aggr_done[which], 4 * b)
                for c in range(c0, c1):
                    dve.bn_stats(stats[which][:, c, :], src[:, c, :]).then_inc(stat_done[which], 1)

            def aggregate(which, b):
                wait(dve, stat_done[which], 4 * b + 4)
                wait_apart(dve, norm_ready[which], 4 * b)
                for c in range(C):
                    dve.bn_aggr(mean_var[which][:, c, :], stats[which][:, c, :]).then_inc(aggr_done[which], 1)

            def lo_half(b, i, bank):
                which, m = i % 2, i // 2
                wait(dve, hi_ready, 4 * b + i + 1)
                dve.scalar_tensor_tensor(lo[:, which, m, :], misc[bank][:, :], bqk[:, which, m:m + 1],
                                         hi[:, which, m, :].bitcast(F32), ALU.add,
                                         ALU.subtract).then_inc(lo_ready, 1)

            def v_copy(b, half, bank):
                wait(dve, v_done, 2 * b + half + 1)
                wait(dve, v_stacked, 4 * b)
                dve.tensor_tensor(v_nat[:, 2 * half:2 * half + 2, :],
                                  misc[bank][:, :].rearrange("p (c d) -> p c d", c=2), bv_all[:, :, :],
                                  ALU.add).then_inc(v_ready, 1)

            def odd_quad(b, pair):
                n = 2 * b + pair
                wait(dve, odd_copied, n + 1)
                wait(dve, attn_ready, n)
                dve.scalar_tensor_tensor(pair_ctx[:, :], pv_bank[:, :], half_hi[:, 0:1], even_ctx[:, :],
                                         ALU.mult, ALU.add).then_inc(odd_out, 1)

            def invert(b, pair):
                n = 2 * b + pair
                wait_apart(dve, sums_in, 32 * n + 32)
                wait_apart(dve, inv_saved, 32 * n)
                dve.reciprocal(inv_small[:, :], sums[:, :]).then_inc(recip_ready, 1)

            def y_half(b, half, bank):
                wait(dve, wo_done, 2 * b + half + 1)
                wait(dve, xbo_ready, b + 1)
                wait(dve, yb_ready, b)
                wait(dve, norm_ready[1], 4 * b)
                dve.tensor_tensor(y[:, 2 * half:2 * half + 2, :],
                                  misc[bank][:, :].rearrange("p (c d) -> p c d", c=2),
                                  x_bo[:, 2 * half:2 * half + 2, :], ALU.add).then_inc(y_ready, 1)
                wait(dve, y_ready, 2 * b + half + 1)
                statistics(1, b, y, 2 * half, 2 * half + 2)

            def out_half(b, half, bank):
                wait(dve, z_done, 2 * b + half + 1)
                wait(dve, yb_ready, b + 1)
                wait(dve, stored, 32 * b)
                dve.tensor_tensor(res[:, 2 * half:2 * half + 2, :],
                                  misc[bank][:, :].rearrange("p (c d) -> p c d", c=2),
                                  y_b[:, 2 * half:2 * half + 2, :], ALU.add).then_inc(out_ready, 1)

            def turn(b, post, prep, load):
                for u in range(UNITS):
                    n = u + LEAD
                    if n < UNITS:
                        row_max(b, n)
                    elif prep:
                        row_max(b + 1, n - UNITS)
                    if prep:
                        if u in (0, 1):
                            if u == 0:
                                wait(dve, x_loaded, 16 * (b + 2))
                            statistics(0, b + 1, x_in, 2 * u, 2 * u + 2)
                        if u == 2:
                            aggregate(0, b + 1)
                    if post:
                        if u == 3:
                            odd_quad(b - 1, 1)
                        if u == 11:
                            invert(b - 1, 1)
                    if prep and u in (6, 10):
                        v_copy(b + 1, (u - 6) // 4, 0)
                    if u == 7:
                        max_halves(b, 1, 1)
                    if prep and u in (15, 17, 19, 21):
                        i = (u - 15) // 2
                        lo_half(b + 1, i, 1 - i % 2)
                    if u == 23:
                        max_halves(b, 2, 1)
                    if post:
                        if u in (25, 27):
                            half = (u - 25) // 2
                            y_half(b - 1, half, half)
                        if u == 28:
                            aggregate(1, b - 1)
                    if u == 35:
                        odd_quad(b, 0)
                    if u == 38:
                        max_halves(b, 3, 1)
                    if post and u in (40, 42):
                        half = (u - 40) // 2
                        out_half(b - 1, half, half)
                    if u == 44:
                        invert(b, 0)
                    if u == 55 and prep:
                        max_halves(b + 1, 0, 1)

            dve.memset(ones[:, :], 1.0).then_inc(dve_set, 1)
            dve.wait_ge(pool_set, 3)
            halves = ident[:, :].rearrange("p (j h d) -> p h j d", j=4, h=2)
            dve.tensor_reduce(half_lo[:, :], halves[:, 0], AX.XY, ALU.add).then_inc(dve_set, 1)
            dve.tensor_reduce(half_hi[:, :], halves[:, 1], AX.XY, ALU.add).then_inc(dve_set, 1)
            dve.wait_ge(x_loaded, 16)
            statistics(0, 0, x_in, 0, 4)
            aggregate(0, 0)
            dve.wait_ge(act_set, 2)
            dve.wait_ge(const_qk, CONSTS_QK)
            for i in range(4):
                lo_half(0, i, 1 - i % 2)
            dve.wait_ge(const_in, CONSTS)
            v_copy(0, 0, 0)
            v_copy(0, 1, 1)
            for n in range(LEAD):
                row_max(0, n)
                if n == 19:
                    max_halves(0, 0, 1)
            turns(dve, turn)
            odd_quad(LAST, 1)
            invert(LAST, 1)
            for half in range(2):
                y_half(LAST, half, half)
            aggregate(1, LAST)
            for half in range(2):
                out_half(LAST, half, half)

        @block.gpsimd
        def _(pool):
            def inverse_root(which, b):
                wait(pool, aggr_done[which], 4 * b + 4)
                wait_apart(pool, norm_ready[which], 4 * b)
                pool.tensor_scalar(var_eps[which][:, :], mean_var[which][:, :, 1], EPS, None,
                                   ALU.add).then_inc(root_step[which], 1)
                wait(pool, root_step[which], 3 * b + 1)
                pool.tensor_tensor(rstd[which][:, :], var_eps[which][:, :], neg_half[:, :],
                                   ALU.pow).then_inc(root_step[which], 1)
                wait(pool, root_step[which], 3 * b + 2)
                pool.tensor_tensor(shift[which][:, :], mean_var[which][:, :, 0], rstd[which][:, :],
                                   ALU.mult).then_inc(root_step[which], 1)
                wait_apart(pool, root_step[which], 3 * b + 3)
                pool.tensor_scalar(shift[which][:, :], shift[which][:, :], -1.0, None,
                                   ALU.mult).then_inc(rstd_ready[which], 1)

            def v_stack(b, g):
                wait(pool, v_ready, 2 * b + 2)
                wait_apart(pool, pv_done, 16 * (b - 1) + 4 * g + 4)
                at = 16 * (g % 2)
                pool.tensor_copy(vs[:, :, 4 * g:4 * g + 4, at:at + 16],
                                 v_nat[:, :, 64 * g:64 * g + 64].rearrange("p c (h d) -> p c h d", h=4))\
                    .then_inc(v_stacked, 1)

            def divide(b, pair):
                n = 2 * b + pair
                wait(pool, inv_ready, 16 * n + 16)
                wait(pool, odd_out, n + 1)
                wait(pool, wo_done, 2 * b)
                pool.tensor_tensor(attnT[:, pair, :], pair_ctx[:, :], inv_sum[:, :],
                                   ALU.mult).then_inc(attn_ready, 1)

            def keep_next(b):
                wait(pool, x_loaded, 16 * (b + 1))
                wait(pool, xbo_ready, b)
                for c in range(C):
                    last = pool.tensor_tensor(x_bo_next[:, c, :], x_in[:, c, :], bo_all[:, :], ALU.add)
                last.then_inc(xbo_next_ready, 1)

            def keep(b):
                wait(pool, xbo_next_ready, b + 1)
                wait_apart(pool, y_ready, 2 * b)
                pool.tensor_copy(x_bo[:, :, :], x_bo_next[:, :, :]).then_inc(xbo_ready, 1)

            def add_b2(b):
                wait(pool, y_ready, 2 * b + 2)
                wait(pool, b2_ready, b + 1)
                wait(pool, out_ready, 2 * b)
                for c in range(C):
                    last = pool.tensor_tensor(y_b[:, c, :], y[:, c, :], b2_all[:, :], ALU.add)
                last.then_inc(yb_ready, 1)

            def b2_parts(b):
                wait(pool, ffn_loaded, 64 * (b + 1))
                wait(pool, b2_done, b)
                pool.tensor_tensor(b2_part[:, :, :], w2_in[:, :, :], b1_in[:, :].unsqueeze(2).to_broadcast([P, OC, D]),
                                   ALU.mult).then_inc(b2_step, 1)
                for k, width in enumerate((4, 2, 1)):
                    wait(pool, b2_step, 4 * b + k + 1)
                    pool.tensor_tensor(b2_part[:, 0:width, :], b2_part[:, 0:width, :],
                                       b2_part[:, width:2 * width, :], ALU.add).then_inc(b2_step, 1)
                wait(pool, b2_step, 4 * b + 4)
                pool.tensor_tensor(b2_part[0:1, 0, :], b2_part[0:1, 0, :], b2_in[:, :],
                                   ALU.add).then_inc(b2_part_ready, 1)

            def turn(b, post, prep, load):
                if prep:
                    inverse_root(0, b + 1)
                if post:
                    v_stack(b, 3)
                    divide(b - 1, 1)
                if prep:
                    v_stack(b + 1, 0)
                if post:
                    inverse_root(1, b - 1)
                    add_b2(b - 1)
                keep(b)
                if prep:
                    v_stack(b + 1, 1)
                    keep_next(b + 1)
                divide(b, 0)
                b2_parts(b)
                if prep:
                    v_stack(b + 1, 2)

            pool.memset(ident[:, :], 0.0).then_inc(pool_set, 1)
            pool.memset(neg_half[:, :], -0.5).then_inc(pool_set, 1)
            pool.wait_ge(pool_set, 1)
            pool.affine_select(out=ident[:, :], in_=ident[:, :], compare_op=ALU.not_equal, fill=1.0, base=0,
                               pattern=[[-1, P]], channel_multiplier=1).then_inc(pool_set, 1)
            pool.wait_ge(pool_set, 3)
            inverse_root(0, 0)
            pool.memset(vs[:, :, :, :], 1.0).then_inc(rows_set, 1)
            pool.wait_ge(rows_set, 1)
            pool.memset(qs[ZROW:MROW, :, :].bitcast(F32), 0.0).then_inc(rows_set, 1)
            pool.wait_ge(rows_set, 2)
            pool.memset(ks[ZROW:MROW, :, :].bitcast(F32), 0.0).then_inc(rows_set, 1)
            pool.wait_ge(rows_set, 3)
            pool.memset(ks[MROW:KS, :, :].bitcast(F32), 1.0).then_inc(rows_set, 1)
            pool.wait_ge(rows_set, 4)
            pool.wait_ge(const_in, CONSTS)
            keep_next(0)
            for g in range(QUADS):
                v_stack(0, g)
            turns(pool, turn)
            divide(LAST, 1)
            inverse_root(1, LAST)
            add_b2(LAST)


def kernel(**inputs):
    import numpy as np
    import concourse.bacc as bacc
    from concourse.bass_utils import run_bass_kernel_spmd

    a = {k: np.asarray(v) for k, v in inputs.items()}
    def by_quad(w):
        return w.reshape((2, 2, 4, HD) + w.shape[1:]).swapaxes(2, 3).reshape(w.shape)

    wo_rows = a["L0_xattn_Wo"].T.reshape(2, 2, 4, HD, D).transpose(0, 2, 1, 3, 4).reshape(D, D)
    arrays = {
        "x": a["x"],
        "ctxT": a["ctx_1024"].transpose(0, 2, 1).reshape(B, F, P, S),
        "wqT": by_quad(a["L0_xattn_Wq"]).T,
        "bq": by_quad(a["L0_xattn_bq"]).reshape(2, P).T,
        "wkT": by_quad(a["L0_xattn_Wk"]).T,
        "bk": by_quad(a["L0_xattn_bk"]).reshape(2, P).T,
        "wvT": a["L0_xattn_Wv"].T,
        "bv": a["L0_xattn_bv"],
        "woT": wo_rows,
        "bo": a["L0_xattn_bo"],
        "w1": a["L0_ffn_W1"],
        "b1": a["L0_ffn_b1"],
        "w2T": a["L0_ffn_W2"].transpose(0, 2, 1),
        "b2": a["L0_ffn_b2"],
    }
    nc = bacc.Bacc("TRN2", target_bir_lowering=False, num_devices=1)
    arrays = {k: np.ascontiguousarray(v) for k, v in arrays.items()}
    args = [nc.dram_tensor(k, v.shape, mybir.dt.from_np(v.dtype), kind="ExternalInput").ap()
            for k, v in arrays.items()]
    args.append(nc.dram_tensor("out", (B, S, D), F32, kind="ExternalOutput").ap())
    xattn_ffn(nc, *args)
    r = run_bass_kernel_spmd(nc, [arrays], core_ids=[0])
    return r.results[0]["out"]
```

```python
from contextlib import ExitStack

import concourse.bass as bass
from concourse import mybir

F32 = mybir.dt.float32
F32R = mybir.dt.float32r
ALU = mybir.AluOpType
ACT = mybir.ActivationFunctionType
AX = mybir.AxisListType

P = 128
B = 8
S = 512
D = 256
H = 16
HD = D // H
INTER = 1024
C = S // P
F = D // P
OC = INTER // P
QUADS = H // 4
UNITS = QUADS * 16
LEAD = 28
FIRST_LEAD = 26
EPS = 1e-5
SCALE = float(HD) ** -0.5
SLOTS = ((0, 0), (1, 0), (0, 1), (1, 1))
ZROW, MROW = 64, 96
KN, KS = MROW, MROW + 2
NATS = 3
LAST = B - 1
B2_STEPS = 11
WQ, WK, WV, WO = range(4)
ATTN_SPLIT = 59
QK_ORDER = ((1, 0), (1, 1), (0, 0), (0, 1))
QK_UNITS = (8, 9, 15, 16, 17, 19, 20, 21)
QK_BANKS = (0, 1, 0, 1)
FIRST_BANKS = (0, 1, 4, 5)
W21_UNITS = ((29, 31, 32, 33, 34, 35, 36, 37), (51, 53, 55, 57, 59, 60, 61, 63))
Z_UNITS = (44, 45, 47, 48)
HALF_UNITS = (10, 17, 20, 22)
LAST_ST = 42
LAST_WO_BANKS = (4, 5, 6, 1)
LAST_SUMS_BANK, LAST_INV_BANK = 2, 3
LAST_YT_BANKS = (4, 5)
LAST_Z_BANKS = (0, 3, 7, 2)


def xattn_ffn(nc, x, ctxT, wqT, bq, wkT, bk, wvT, bv, woT, bo, w1, b1, w2T, b2, out):
    with ExitStack() as stack:
        def sb(name, shape, dt=F32):
            return stack.enter_context(nc.sbuf_tensor(name, shape, dt))

        def pb(name):
            return stack.enter_context(nc.psum_tensor(name, [P, S], F32))

        def sem(name):
            return stack.enter_context(nc.semaphore(name))

        ident = sb("ident", [P, P])
        ones = sb("ones", [P, P])
        pick = sb("pick", [P, 4, 2])
        half_lo = sb("half_lo", [P, 1])
        half_hi = sb("half_hi", [P, 1])
        neg_half = sb("neg_half", [P, C])
        w_hi = sb("w_hi", [P, 4, F, D], F32R)
        w_lo = sb("w_lo", [P, 4, F, D], F32R)
        bq_in = sb("bq_in", [P, 2])
        bqk = sb("bqk", [P, 2, 2])
        bv_all = sb("bv_all", [P, 1, D])
        bo_all = sb("bo_all", [P, D])
        x_in = sb("x_in", [P, C, D])
        ctx_hi = sb("ctx_hi", [P, F, S], F32R)
        ctx_lo = sb("ctx_lo", [P, F, S], F32R)
        ctx_in = sb("ctx_in", [P, F, S])
        normed = sb("normed", [P, C, D])
        normedT_hi = sb("normedT_hi", [P, F, S], F32R)
        normedT_lo = sb("normedT_lo", [P, F, S], F32R)
        stats = [sb(f"stats{i}", [P, C, 6]) for i in range(2)]
        mean_var = [sb(f"mean_var{i}", [P, C, 2]) for i in range(2)]
        var_eps = [sb(f"var_eps{i}", [P, C]) for i in range(2)]
        rstd = [sb(f"rstd{i}", [P, C]) for i in range(2)]
        shift = [sb(f"shift{i}", [P, C]) for i in range(2)]
        hi = sb("hi", [P, 2, 2, S], F32R)
        lo = sb("lo", [P, 2, 2, S], F32R)
        qs = sb("qs", [P, H, S], F32R)
        ks = sb("ks", [P, H, S], F32R)
        v_nat = sb("v_nat", [P, C, D])
        vs = sb("vs", [P, C, H, 32])
        neg_max = sb("neg_max", [P, 2, 16])
        max_hi = sb("max_hi", [16, P], F32R)
        max_lo = sb("max_lo", [16, P], F32R)
        probs = [sb(f"probs{i}", [P, 4, S]) for i in range(2)]
        even_ctx = sb("even_ctx", [P, S])
        even_sum = sb("even_sum", [P, S])
        pair_ctx = sb("pair_ctx", [P, S])
        odd_sum = sb("odd_sum", [P, S])
        sums = sb("sums", [P, 32])
        inv_small = sb("inv_small", [P, 32])
        inv_sum = sb("inv_sum", [P, S])
        attnT_hi = sb("attnT_hi", [P, 2, S], F32R)
        attnT_lo = sb("attnT_lo", [P, 2, S], F32R)
        y = sb("y", [P, C, D])
        w1_in = sb("w1_in", [P, OC, D])
        w2_in = sb("w2_in", [P, OC, D])
        b1_in = sb("b1_in", [P, OC])
        b2_in = sb("b2_in", [1, D])
        b2_part = sb("b2_part", [P, 5, D])
        b2_all = sb("b2_all", [P, D])
        w21_half = sb("w21_half", [P, D])
        w21_hi = sb("w21_hi", [P, F, D], F32R)
        w21_lo = sb("w21_lo", [P, F, D], F32R)

        inv_dram = nc.dram_tensor("inv_dram", (4, 2, S), F32, kind="Internal").ap()

        w_in = probs[0][:, :, :].rearrange("p w (f d) -> p w f d", f=F)

        st_bank = [pb("st0"), pb("st1")]
        nat_bank = [pb(f"nat{i}") for i in range(NATS)]
        pv_bank = pb("pv")
        misc = [pb("misc0"), pb("misc1")]
        misc += st_bank + nat_bank + [pv_bank]

        const_qk = sem("const_qk")
        const_in = sem("const_in")
        x_loaded = sem("x_loaded")
        ctx_loaded = sem("ctx_loaded")
        ffn_loaded = sem("ffn_loaded")
        stacked = [sem(f"stacked{g}") for g in range(QUADS)]
        max_rows = sem("max_rows")
        sums_in = sem("sums_in")
        inv_saved = sem("inv_saved")
        inv_ready = sem("inv_ready")
        stored = sem("stored")
        pool_set = sem("pool_set")
        rows_set = sem("rows_set")
        dve_set = sem("dve_set")
        act_set = sem("act_set")
        st_done = sem("st_done")
        nat_done = sem("nat_done")
        pv_done = sem("pv_done")
        maxT_done = sem("maxT_done")
        xT_done = sem("xT_done")
        qk_done = sem("qk_done")
        v_done = sem("v_done")
        wo_done = sem("wo_done")
        b2_done = sem("b2_done")
        yT_done = sem("yT_done")
        z_done = sem("z_done")
        w21_done = sem("w21_done")
        exp_done = sem("exp_done")
        xT_ready = sem("xT_ready")
        yT_ready = sem("yT_ready")
        hi_ready = sem("hi_ready")
        xT_hi = sem("xT_hi")
        yT_hi = sem("yT_hi")
        ctx_hi_ready = sem("ctx_hi_ready")
        attn_hi_ready = sem("attn_hi_ready")
        w21_hi_ready = sem("w21_hi_ready")
        w_hi_ready = sem("w_hi_ready")
        w_ready = sem("w_ready")
        even_out = sem("even_out")
        even_masked = sem("even_masked")
        odd_copied = sem("odd_copied")
        b2_ready = sem("b2_ready")
        w21_first = sem("w21_first")
        w21_ready = sem("w21_ready")
        max_done = sem("max_done")
        lo_ready = sem("lo_ready")
        maxhi_ready = sem("maxhi_ready")
        max_ready = sem("max_ready")
        v_ready = sem("v_ready")
        odd_out = sem("odd_out")
        recip_ready = sem("recip_ready")
        y_ready = sem("y_ready")
        out_ready = sem("out_ready")
        stat_done = [sem("xstat_done"), sem("ystat_done")]
        aggr_done = [sem("xaggr_done"), sem("yaggr_done")]
        root_step = [sem("xroot_step"), sem("yroot_step")]
        rstd_ready = [sem("xrstd_ready"), sem("yrstd_ready")]
        norm_ready = [sem("xnorm_ready"), sem("ynorm_ready")]
        v_stacked = sem("v_stacked")
        attn_ready = sem("attn_ready")
        ctx_ready = sem("ctx_ready")
        divided = sem("divided")
        y_loaded = sem("y_loaded")
        xbo_ready = sem("xbo_ready")
        yb_ready = sem("yb_ready")
        b2_step = sem("b2_step")
        b2_part_ready = sem("b2_part_ready")

        last_even = sem("last_even")
        last_comb = sem("last_comb")
        last_sums = sem("last_sums")
        last_recip = sem("last_recip")
        last_inv = sem("last_inv")
        last_attn = sem("last_attn")
        last_wo = sem("last_wo")
        last_y = sem("last_y")
        last_norm = sem("last_norm")
        last_z = sem("last_z")

        passed = {e.engine: sem(f"passed_{n}") for e, n in
                  ((nc.sync, "sp"), (nc.vector, "dve"), (nc.gpsimd, "pool"))}

        def nat_of(n):
            return nat_bank[n % NATS if n < UNITS - 1 else 1]

        def st_of(u, prep):
            return (st_bank + nat_bank)[u % 3] if not prep and u >= LAST_ST else st_bank[u % 2]

        def nats_of(b, u, post, prep):
            if not post and FIRST_LEAD + 2 * u < u + LEAD:
                return [(b, FIRST_LEAD + 2 * u + i) for i in range(2)]
            n = u + LEAD
            if n < UNITS:
                return [(b, n)]
            return [(b + 1, n - UNITS)] if prep else []

        CONSTS_QK = 4 * 16
        CONSTS = 4 * 16

        def wait(eng, s, value):
            if not (isinstance(value, int) and value <= 0):
                eng.wait_ge(s, value)

        def wait_apart(eng, s, value):
            wait(eng, s, value)
            if not isinstance(value, int):
                eng.sem_inc(passed[eng.engine], 1)

        def turns(eng, turn):
            turn(0, False, True, True)
            turn(1, True, True, True)
            with eng.Fori(2, B - 2) as b:
                turn(b, True, True, True)
            turn(B - 2, True, True, False)
            turn(B - 1, True, False, False)

        block = stack.enter_context(nc.Block())

        @block.sync
        def _(sp):
            def load_x(b):
                sp.dma_start(x_in[:, :, :], x[b].rearrange("(p c) d -> p c d", c=C)).then_inc(x_loaded, 16)

            def load_ctx(b):
                sp.dma_start(ctx_in[:, :, :], ctxT[b].rearrange("f p s -> p f s")).then_inc(ctx_loaded, 16)

            def load_y(b):
                wait_apart(sp, stored, 32 * b)
                sp.dma_start(y[:, :, :], x[b].rearrange("(p c) d -> p c d", c=C)).then_inc(y_loaded, 16)

            def load_ffn(b):
                sp.dma_start(w1_in[:, :, :], w1[b].rearrange("(p o) d -> p o d", o=OC)).then_inc(ffn_loaded, 16)
                sp.dma_start(w2_in[:, :, :], w2T[b].rearrange("(p o) d -> p o d", o=OC)).then_inc(ffn_loaded, 16)
                sp.dma_start(b1_in[:, :], b1[b].rearrange("(p o) -> p o", o=OC)).then_inc(ffn_loaded, 16)
                sp.dma_start(b2_in[:, :], b2[b].rearrange("(a d) -> a d", a=1)).then_inc(ffn_loaded, 16)

            def stack_quad(b, g):
                wait_apart(sp, st_done, UNITS * (b - 1) + 16 * g + 16)
                rows = slice(64 * (g % 2), 64 * (g % 2) + 64)
                for which, dst in ((1, ks), (0, qs)):
                    wait_apart(sp, lo_ready, 4 * b + QK_ORDER.index((which, g // 2)) + 1)
                    for s, halves in enumerate(SLOTS):
                        src = (hi, lo)[halves[which]]
                        sp.dma_start(dst[16 * s:16 * s + 16, 4 * g:4 * g + 4, :].bitcast(F32),
                                     src[rows, which, g // 2, :].bitcast(F32)).then_inc(stacked[g], 16)

            def store_max(b, g):
                wait_apart(sp, max_ready, 4 * b + g + 1)
                wait_apart(sp, st_done, UNITS * (b - 1) + 16 * g + 16)
                for r, src in enumerate((max_hi, max_lo)):
                    dst = qs[MROW + r:MROW + r + 1, 4 * g:4 * g + 4, :].bitcast(F32)
                    sp.dma_start(dst.rearrange("a h (c t) -> a (h c) t", c=C),
                                 src[:, :].bitcast(F32)).then_inc(max_rows, 16)

            def store_out(b, half):
                wait_apart(sp, out_ready, 2 * b + half + 1)
                sp.dma_start(out[b].rearrange("(p c) d -> p c d", c=C)[:, 2 * half:2 * half + 2, :],
                             y[:, 2 * half:2 * half + 2, :]).then_inc(stored, 16)

            def gather_sums(b, pair):
                n = 2 * b + pair
                wait_apart(sp, even_out, n + 1)
                wait_apart(sp, odd_copied, n + 1)
                wait_apart(sp, recip_ready, n)
                sp.dma_start(sums[0:64, :], even_sum[16:P:32, :]).then_inc(sums_in, 16)
                sp.dma_start(sums[64:P, :], odd_sum[0:P:32, :]).then_inc(sums_in, 16)

            def save_inverse(b, pair):
                n = 2 * b + pair
                wait_apart(sp, recip_ready, n + 1)
                wait_apart(sp, inv_ready, 16 * n)
                for t in range(2):
                    sp.dma_start(inv_dram[:, t, :].rearrange("j (k i) -> j k i", i=32),
                                 inv_small[64 * t:64 * t + 64, :]).then_inc(inv_saved, 16)

            def spread_inverse(b, pair):
                n = 2 * b + pair
                wait_apart(sp, inv_saved, 32 * n + 32)
                wait_apart(sp, attn_ready, n)
                sp.dma_start(inv_sum[:, :],
                             inv_dram.rearrange("j t s -> (j t) s").unsqueeze(1).to_broadcast([8, HD, S]))\
                    .then_inc(inv_ready, 16)

            def turn(b, post, prep, load):
                if post:
                    gather_sums(b - 1, 1)
                    stack_quad(b, 3)
                store_max(b, 1)
                if post:
                    save_inverse(b - 1, 1)
                    spread_inverse(b - 1, 1)
                    wait_apart(sp, w21_done, 2 * b)
                    wait_apart(sp, b2_part_ready, b)
                    load_ffn(b)
                if prep:
                    stack_quad(b + 1, 0)
                store_max(b, 2)
                if load:
                    wait_apart(sp, norm_ready[0], 4 * (b + 2))
                    load_x(b + 2)
                    wait_apart(sp, v_done, 2 * (b + 2))
                    wait_apart(sp, qk_done, 4 * (b + 2))
                    load_ctx(b + 2)
                if prep:
                    stack_quad(b + 1, 1)
                gather_sums(b, 0)
                store_max(b, 3)
                save_inverse(b, 0)
                if post:
                    store_out(b - 1, 0)
                spread_inverse(b, 0)
                if post:
                    store_out(b - 1, 1)
                load_y(b)
                if prep:
                    stack_quad(b + 1, 2)
                    store_max(b + 1, 0)

            def load_w(which, src, done):
                sp.dma_start(w_in[:, which], src.rearrange("(f p) d -> p f d", p=P)).then_inc(done, 16)

            load_x(0)
            load_ctx(0)
            load_w(WK, wkT, const_qk)
            sp.dma_start(bqk[:, 1, :], bk).then_inc(const_qk, 16)
            load_w(WQ, wqT, const_qk)
            sp.dma_start(bq_in[:, :], bq).then_inc(const_qk, 16)
            load_w(WV, wvT, const_in)
            sp.dma_start(bv_all[:, 0, :], bv.partition_broadcast(P)).then_inc(const_in, 16)
            sp.dma_start(bo_all[:, :], bo.partition_broadcast(P)).then_inc(const_in, 16)
            load_w(WO, woT, const_in)
            load_ffn(0)
            for g in range(QUADS):
                if g == 2:
                    sp.wait_ge(norm_ready[0], 4)
                    load_x(1)
                    sp.wait_ge(v_done, 2)
                    sp.wait_ge(qk_done, 4)
                    load_ctx(1)
                if g == 3:
                    store_max(0, 0)
                stack_quad(0, g)
            turns(sp, turn)
            store_out(LAST, 0)
            store_out(LAST, 1)
            sp.wait_ge(stored, 32 * B)

        @block.tensor
        def _(pe):
            mm = nc.tensor.matmul

            def stay_warm(n, bank):
                for _ in range(n):
                    mm(misc[bank][:, 0:P], ones[:, :], ident[:, :], start=True, stop=True)

            def nat(b, n):
                g, j, c = n // 16, n % 16 // 4, n % 4
                h = 4 * g + j
                if n % 16 == 0:
                    wait(pe, stacked[g], 128 * (b + 1))
                wait(pe, max_done, UNITS * b + {0: -3, 1: 0, 2: -1, UNITS - 1: n - 1}.get(n, n - 2))
                mm(nat_of(n)[:, :], qs[0:KN, h, c * P:(c + 1) * P], ks[0:KN, h, :],
                   start=True, stop=True).then_inc(nat_done, 1)

            def st(b, u, prep):
                g, kc, j = u // 16, u % 16 // 4, u % 4
                h = 4 * g + j
                if u % 16 == 0:
                    wait(pe, max_rows, 32 * (4 * b + g + 1))
                wait(pe, exp_done, UNITS * b + u - (2 if not prep and u >= LAST_ST + 2 else 1))
                mm(st_of(u, prep)[:, :], ks[0:KS, h, kc * P:(kc + 1) * P], qs[0:KS, h, :],
                   start=True, stop=True).then_inc(st_done, 1)

            def pv(b, n):
                g, kc = n // 4, n % 4
                if kc == 0:
                    wait(pe, v_stacked, 4 * b + g + 1)
                    pair = 2 * b + g // 2
                    if g % 2:
                        wait(pe, even_out, pair + 1)
                    else:
                        wait(pe, odd_out, pair)
                wait(pe, exp_done, UNITS * b + 4 * n + 4)
                for j in range(4):
                    last = mm(pv_bank[32 * j:32 * j + 32, :], vs[:, kc, 4 * g + j, :],
                              probs[n % 2][:, j, :], start=(kc == 0), stop=(kc == 3),
                              tile_position=(0, 32 * j), skip_group_check=True)
                last.then_inc(pv_done, 1)

            def product(dst, left, right, start=True, stop=True):
                for n, (i, j) in enumerate(((0, 0), (1, 0), (0, 1))):
                    last = mm(dst, left[i], right[j], start=start and n == 0, stop=stop and n == 2)
                return last

            def halves(pair, *index):
                return [t[index] for t in pair]

            ALL = slice(None)

            def transposeT(bank, f, done):
                for c in range(C):
                    last = nc.tensor.transpose(misc[bank][:, c * P:(c + 1) * P],
                                               normed[:, c, f * P:(f + 1) * P], ident[:, :])
                last.then_inc(done, 1)

            def xT(b, f, bank):
                wait(pe, norm_ready[0], 4 * b + 4)
                transposeT(bank, f, xT_done)

            def yT(b, f, bank):
                wait(pe, norm_ready[1], 4 * b + 4)
                transposeT(bank, f, yT_done)

            def maxT(b, g, bank):
                wait(pe, max_done, UNITS * b + 16 * g + 16)
                nc.tensor.transpose(misc[bank][0:16, 0:P], neg_max[:, g % 2, :],
                                    ident[:, :]).then_inc(maxT_done, 1)

            def qk(b, i, bank, f):
                which, m = QK_ORDER[i]
                src, w = ((normedT_hi, normedT_lo), WQ) if which == 0 else ((ctx_hi, ctx_lo), WK)
                last = product(misc[bank][:, :], halves((w_hi, w_lo), ALL, w, f, slice(m * P, (m + 1) * P)),
                               halves(src, ALL, f, ALL), start=(f == 0), stop=(f == F - 1))
                if f == F - 1:
                    last.then_inc(qk_done, 1)

            def v(b, c, bank):
                if c == 0:
                    wait(pe, ctx_ready, b + 1)
                for f in range(F):
                    last = product(misc[bank][:, (c % 2) * D:(c % 2 + 1) * D],
                                   halves((ctx_hi, ctx_lo), ALL, f, slice(c * P, (c + 1) * P)),
                                   halves((w_hi, w_lo), ALL, WV, f, ALL), start=(f == 0), stop=(f == F - 1))
                if c % 2:
                    last.then_inc(v_done, 1)

            def wo_part(dst, c, f):
                return product(dst, halves((attnT_hi, attnT_lo), ALL, f, slice(c * P, (c + 1) * P)),
                               halves((w_hi, w_lo), ALL, WO, f, ALL), start=(f == 0), stop=(f == F - 1))

            def wo_(b, c, bank):
                if c == 0:
                    wait(pe, attn_ready, 2 * b + 2)
                for f in range(F):
                    last = wo_part(misc[bank][:, (c % 2) * D:(c % 2 + 1) * D], c, f)
                if c % 2:
                    last.then_inc(wo_done, 1)

            def b2sum(b, bank):
                wait(pe, b2_part_ready, b + 1)
                mm(misc[bank][:, 0:D], ones[:, :], b2_part[:, 0, :], start=True, stop=True).then_inc(b2_done, 1)

            def z_part(dst, c, f, start):
                return product(dst, halves((normedT_hi, normedT_lo), ALL, f, slice(c * P, (c + 1) * P)),
                               halves((w21_hi, w21_lo), ALL, f, ALL), start=start, stop=(f == F - 1))

            def z(b, c, bank):
                if c == 0:
                    wait(pe, yT_ready, 2 * b + 2)
                    wait(pe, w21_ready, b + 1)
                for f in range(F):
                    last = z_part(misc[bank][:, (c % 2) * D:(c % 2 + 1) * D], c, f, f == 0)
                if c % 2:
                    last.then_inc(z_done, 1)

            def w21_part(b, n, bank):
                f, o = n // OC, n % OC
                if n == 0:
                    wait(pe, ffn_loaded, 64 * (b + 1))
                last = mm(misc[bank][:, 0:D], w1_in[:, o, f * P:(f + 1) * P], w2_in[:, o, :],
                          start=(o == 0), stop=(o == OC - 1))
                if o == OC - 1:
                    last.then_inc(w21_done, 1)

            def jobs(b, u, post, prep):
                if prep:
                    if u == 0:
                        wait(pe, max_ready, 4 * b + 1)
                        wait(pe, w21_first, b + (0 if post else 1))
                    if u in (0, 1):
                        v(b + 1, u, 1)
                    if u == 3:
                        wait(pe, w21_ready, b)
                    if u in (3, 4):
                        v(b + 1, u - 1, 0)
                if u == 7:
                    wait(pe, max_ready, 4 * b + 1)
                    wait(pe, v_ready, 2 * b + 3 if prep else 0)
                    maxT(b, 1, 1)
                if prep:
                    if u == 11:
                        wait(pe, max_ready, 4 * b + 2)
                        xT(b + 1, 0, 1)
                    if u == 12:
                        wait(pe, lo_ready, 4 * b + 5)
                        xT(b + 1, 1, 0)
                    if u in QK_UNITS:
                        i, f = QK_UNITS.index(u) // 2, QK_UNITS.index(u) % 2
                        if u == QK_UNITS[0]:
                            wait(pe, v_ready, 2 * b + 4)
                        if i in (1, 2) and f == 0:
                            wait(pe, xT_ready, 2 * b + 2 + i)
                        if i == 3 and f == 0:
                            wait(pe, lo_ready, 4 * b + 6)
                        qk(b + 1, i, QK_BANKS[i], f)
                if u == 23:
                    wait(pe, lo_ready, 4 * b + 7 if prep else 0)
                    wait(pe, w21_ready, b)
                    maxT(b, 2, 0)
                if post:
                    if u == 24:
                        wait(pe, lo_ready, 4 * b + 8 if prep else 0)
                        wait(pe, max_ready, 4 * b + 2)
                    if u in (24, 25):
                        wo_(b - 1, u - 24, 1)
                    if u == 27:
                        wait(pe, max_ready, 4 * b + 3)
                    if u in (27, 28):
                        wo_(b - 1, u - 25, 0)
                    if u == 31:
                        wait(pe, y_ready, 2 * b)
                        b2sum(b - 1, 0)
                if post and u in W21_UNITS[0]:
                    n = W21_UNITS[0].index(u)
                    if n == 0:
                        wait(pe, y_ready, 2 * b - 1)
                    w21_part(b, n, 1)
                if post:
                    if u == 36:
                        wait(pe, b2_ready, b)
                        yT(b - 1, 0, 0)
                    if u == 39:
                        wait(pe, w21_first, b + 1)
                        yT(b - 1, 1, 1)
                if u == 40:
                    wait(pe, yT_ready, 2 * b - 1 if post else 0)
                    wait(pe, max_ready, 4 * b + 3)
                    maxT(b, 3, 0)
                if post and u in Z_UNITS:
                    c = Z_UNITS.index(u)
                    if c == 0:
                        wait(pe, max_ready, 4 * b + 4)
                    z(b - 1, c, c // 2)
                if u in W21_UNITS[1]:
                    n = W21_UNITS[1].index(u)
                    if n == 0:
                        wait(pe, out_ready, 2 * b - 1 if post else 0)
                        wait(pe, max_ready, 4 * b + 4)
                    w21_part(b, OC + n, 0)
                if u == 54 and prep:
                    wait(pe, out_ready, 2 * b if post else 0)
                    wait(pe, w21_first, b + 1)
                    maxT(b + 1, 0, 1)

            def turn(b, post, prep, load):
                for u in range(UNITS):
                    st(b, u, prep)
                    for row, n in nats_of(b, u, post, prep):
                        nat(row, n)
                    if u % 4 == 2:
                        if u > 4:
                            pv(b, u // 4 - 1)
                        elif post:
                            pv(b - 1, 15)
                    jobs(b, u, post, prep)

            pe.wait_ge(pool_set, 3)
            pe.wait_ge(dve_set, 1)
            stay_warm(24, 7)
            pe.wait_ge(ctx_ready, 1)
            pe.wait_ge(w_ready, 1)
            for f in range(F):
                qk(0, 0, FIRST_BANKS[0], f)
            xT(0, 0, 2)
            xT(0, 1, 3)
            for f in range(F):
                qk(0, 1, FIRST_BANKS[1], f)
            pe.wait_ge(xT_ready, 2)
            pe.wait_ge(w_ready, 2)
            for i in (2, 3):
                for f in range(F):
                    qk(0, i, FIRST_BANKS[i], f)
            pe.wait_ge(w_ready, 3)
            for c in range(C):
                v(0, c, 6 + c // 2)
            pe.wait_ge(lo_ready, 4)
            pe.wait_ge(rows_set, 2)
            pe.wait_ge(dve_set, 5)
            pe.wait_ge(act_set, 1)
            pe.wait_ge(v_ready, 2)
            for n in range(FIRST_LEAD):
                nat(0, n)
                if n < OC:
                    w21_part(0, n, 1)
                if n == 17:
                    maxT(0, 0, 0)
            pe.wait_ge(rows_set, 4)
            turns(pe, turn)
            pv(LAST, 15)
            pe.wait_ge(last_comb, 1)
            pe.wait_ge(exp_done, UNITS * B)
            for c in range(C):
                last = mm(misc[LAST_SUMS_BANK][:, 8 * c:8 * c + 8], odd_sum[:, c * P:(c + 1) * P],
                          pick[:, :, :].rearrange("p j t -> p (j t)"), start=True, stop=True)
            last.then_inc(last_sums, 1)
            pe.wait_ge(attn_ready, 2 * LAST + 1)
            pe.wait_ge(max_done, UNITS * B)
            pe.wait_ge(out_ready, 2 * LAST)
            for c in range(C):
                wo_part(misc[LAST_WO_BANKS[c]][:, 0:D], c, 0)
            pe.wait_ge(last_recip, 1)
            for c in range(C):
                last = mm(misc[LAST_INV_BANK][:, c * P:(c + 1) * P],
                          even_sum[:, c * P:(c + 1) * P], ident[:, :], start=True, stop=True)
            last.then_inc(last_inv, 1)
            pe.wait_ge(odd_out, 2 * B)
            stay_warm(10, 7)
            pe.wait_ge(last_attn, 1)
            for c in range(C):
                wo_part(misc[LAST_WO_BANKS[c]][:, 0:D], c, 1).then_inc(last_wo, 1)
            pe.wait_ge(b2_part_ready, B)
            pe.wait_ge(w21_ready, B)
            for c in range(C):
                mm(misc[LAST_Z_BANKS[c]][:, 0:D], ones[:, :], b2_part[:, 0, :], start=True, stop=False)
            pe.wait_ge(last_y, C)
            stay_warm(15, LAST_YT_BANKS[0])
            pe.wait_ge(norm_ready[1], 4 * LAST + 1)
            pe.wait_ge(last_norm, 3)
            for f in range(F):
                transposeT(LAST_YT_BANKS[f], f, yT_done)
            stay_warm(6, 6)
            for c in range(C):
                for f in range(F):
                    if c == 0:
                        pe.wait_ge(yT_ready, 2 * LAST + f + 1)
                    last = z_part(misc[LAST_Z_BANKS[c]][:, 0:D], c, f, False)
                last.then_inc(last_z, 1)

        @block.scalar
        def _(act):
            def exp(b, u, prep):
                kc, j = u // 4, u % 4
                wait(act, st_done, UNITS * b + u + 1)
                if j == 0:
                    wait(act, pv_done, 16 * b + kc - 1)
                act.activation(probs[kc % 2][:, j, :], st_of(u, prep)[:, :], ACT.Exp).then_inc(exp_done, 1)

            def xT_copy(b, f, bank):
                wait(act, xT_done, 2 * b + f + 1)
                wait(act, z_done, 2 * (b - 2))
                wait(act, qk_done, 4 * b)
                act.activation(normedT_hi[:, f, :], misc[bank][:, :], ACT.Copy).then_inc(xT_hi, 1)

            def yT_copy(b, f, bank, prep):
                wait(act, yT_done, 2 * b + f + 1)
                wait(act, qk_done, 4 * (b + 2) if prep else 0)
                wait(act, z_done, 2 * b)
                act.activation(normedT_hi[:, f, :], misc[bank][:, :], ACT.Copy).then_inc(yT_hi, 1)

            def hi_half(b, i, bank):
                which, m = QK_ORDER[i]
                wait(act, qk_done, 4 * b + i + 1)
                for g in (2 * m, 2 * m + 1):
                    wait(act, stacked[g], 128 * b)
                act.activation(hi[:, which, m, :], misc[bank][:, :], ACT.Identity,
                               bias=bqk[:, which, m:m + 1]).then_inc(hi_ready, 1)

            def even_quad(b, pair):
                n = 2 * b + pair
                wait(act, pv_done, 16 * b + 8 * pair + 4)
                wait(act, odd_out, n)
                wait(act, sums_in, 32 * n)
                act.activation(even_sum[:, :], pv_bank[:, :], ACT.Copy).then_inc(even_out, 1)

            def mask_even(b, pair):
                n = 2 * b + pair
                wait(act, even_out, n + 1)
                act.activation(even_ctx[:, :], even_sum[:, :], ACT.Copy,
                               scale=half_lo[:, 0:1]).then_inc(even_masked, 1)

            def odd_quad(b, pair):
                n = 2 * b + pair
                wait(act, pv_done, 16 * b + 8 * pair + 8)
                wait(act, sums_in, 32 * n)
                act.activation(odd_sum[:, :], pv_bank[:, :], ACT.Copy).then_inc(odd_copied, 1)

            def normalise(which, b, src, c0, c1):
                wait(act, rstd_ready[which], b + 1)
                for c in range(c0, c1):
                    act.activation(normed[:, c, :], src[:, c, :], ACT.Identity, bias=shift[which][:, c:c + 1],
                                   scale=rstd[which][:, c:c + 1]).then_inc(norm_ready[which], 1)

            def b2_copy(b):
                wait(act, b2_done, b + 1)
                wait(act, yb_ready, b)
                act.activation(b2_all[:, :], misc[0][:, 0:D], ACT.Copy).then_inc(b2_ready, 1)

            def w21_copy_first(b):
                wait(act, w21_done, 2 * b + 1)
                wait(act, w21_ready, b)
                act.activation(w21_half[:, :], misc[1][:, 0:D], ACT.Copy).then_inc(w21_first, 1)

            def w21_copy(b):
                wait(act, z_done, 2 * b)
                wait(act, w21_first, b + 1)
                act.activation(w21_hi[:, 0, :], w21_half[:, :], ACT.Copy).then_inc(w21_hi_ready, 1)
                wait(act, w21_done, 2 * b + 2)
                act.activation(w21_hi[:, 1, :], misc[0][:, 0:D], ACT.Copy).then_inc(w21_hi_ready, 1)

            def ctx_split(b):
                wait(act, ctx_loaded, 16 * (b + 1))
                wait(act, v_done, 2 * b)
                wait(act, qk_done, 4 * b)
                act.activation(ctx_hi[:, :, :], ctx_in[:, :, :], ACT.Copy).then_inc(ctx_hi_ready, 1)

            def attn_split(b, pair):
                n = 2 * b + pair
                wait(act, divided, n + 1)
                wait(act, wo_done, 2 * b)
                act.activation(attnT_hi[:, pair, :], pair_ctx[:, :], ACT.Copy).then_inc(attn_hi_ready, 1)

            def turn(b, post, prep, load):
                for u in range(UNITS):
                    exp(b, u, prep)
                    if post:
                        if u == 0:
                            w21_copy(b - 1)
                        if u == 3:
                            odd_quad(b - 1, 1)
                    if prep:
                        if u == 6:
                            wait(act, xT_done, 2 * (b + 1))
                            wait(act, yT_done, 2 * (b - 1) if post else 0)
                        if u in (6, 7):
                            normalise(0, b + 1, x_in, 2 * (u - 6), 2 * (u - 6) + 2)
                        if u in (12, 13):
                            f = u - 12
                            xT_copy(b + 1, f, 1 - f)
                        if u in HALF_UNITS:
                            i = HALF_UNITS.index(u)
                            hi_half(b + 1, i, QK_BANKS[i])
                    if u in (19, 51):
                        even_quad(b, u // 32)
                    if u in (22, 54):
                        mask_even(b, u // 32)
                    if not prep and u == 57:
                        wait(act, sums_in, 32 * (2 * b + 1))
                        act.activation(odd_sum[:, :], even_sum[:, :], ACT.Copy,
                                       scale=half_hi[:, 0:1]).then_inc(last_even, 1)
                    if post:
                        if u == 32:
                            b2_copy(b - 1)
                        if u == 33:
                            wait(act, xT_done, 2 * (b + 2) if prep else 0)
                            wait(act, yT_done, 2 * (b - 1))
                        if u in (33, 34):
                            normalise(1, b - 1, y, 2 * (u - 33), 2 * (u - 33) + 2)
                        if u == 37:
                            yT_copy(b - 1, 0, 0, prep)
                    if u == 35:
                        odd_quad(b, 0)
                    if post and u == 38:
                        w21_copy_first(b)
                    if post and u == 40:
                        yT_copy(b - 1, 1, 1, prep)
                    if post and u == 21:
                        attn_split(b - 1, 1)
                    if load and u == 43:
                        ctx_split(b + 2)
                    if u == ATTN_SPLIT:
                        attn_split(b, 0)

            act.wait_ge(dve_set, 1)
            act.activation(ks[ZROW:MROW, 8:H, :], ones[ZROW:MROW, 0:1].unsqueeze(2).to_broadcast([MROW - ZROW, 8, S]),
                           ACT.Copy, scale=0.0).then_inc(act_set, 1)
            act.wait_ge(const_qk, CONSTS_QK)
            act.activation(w_hi[:, WK], w_in[:, WK], ACT.Copy).then_inc(w_hi_ready, 1)
            ctx_split(0)
            act.activation(w_hi[:, WQ], w_in[:, WQ], ACT.Copy, scale=SCALE).then_inc(w_hi_ready, 1)
            act.activation(bqk[:, 0, :], bq_in[:, :], ACT.Copy, scale=SCALE).then_inc(act_set, 1)
            normalise(0, 0, x_in, 0, C)
            act.wait_ge(act_set, 2)
            hi_half(0, 0, FIRST_BANKS[0])
            xT_copy(0, 0, 2)
            xT_copy(0, 1, 3)
            hi_half(0, 1, FIRST_BANKS[1])
            act.wait_ge(const_in, CONSTS)
            act.activation(w_hi[:, WV], w_in[:, WV], ACT.Copy).then_inc(w_hi_ready, 1)
            hi_half(0, 2, FIRST_BANKS[2])
            act.activation(w_hi[:, WO], w_in[:, WO], ACT.Copy).then_inc(w_hi_ready, 1)
            hi_half(0, 3, FIRST_BANKS[3])
            w21_copy_first(0)
            act.wait_ge(dve_set, 4)
            act.wait_ge(w_ready, 4)
            act.wait_ge(ctx_loaded, 32)
            ctx_split(1)
            turns(act, turn)
            w21_copy(LAST)
            attn_split(LAST, 1)
            act.wait_ge(yT_done, 2 * LAST)
            normalise(1, LAST, y, 3, C)
            for f in range(F):
                yT_copy(LAST, f, LAST_YT_BANKS[f], False)

        @block.vector
        def _(dve):
            def row_max(b, n):
                g = n // 16
                wait(dve, nat_done, UNITS * b + n + 1)
                if n % 16 == 0:
                    wait(dve, maxT_done, 4 * b + g - 1)
                dve.tensor_reduce(neg_max[:, g % 2, n % 16:n % 16 + 1], nat_of(n)[:, :], AX.X, ALU.max,
                                  negate=True).then_inc(max_done, 1)

            def max_halves(b, g, bank):
                wait(dve, maxT_done, 4 * b + g + 1)
                wait(dve, max_rows, 32 * (4 * b + g))
                dve.tensor_copy(max_hi[:, :], misc[bank][0:16, 0:P]).then_inc(maxhi_ready, 1)
                wait(dve, maxhi_ready, 4 * b + g + 1)
                dve.tensor_tensor(max_lo[:, :], misc[bank][0:16, 0:P], max_hi[:, :].bitcast(F32),
                                  ALU.subtract).then_inc(max_ready, 1)

            def statistics(which, b, src, c0, c1):
                wait(dve, aggr_done[which], 4 * b)
                for c in range(c0, c1):
                    dve.bn_stats(stats[which][:, c, :], src[:, c, :]).then_inc(stat_done[which], 1)

            def aggregate(which, b):
                wait(dve, stat_done[which], 4 * b + 4)
                wait_apart(dve, norm_ready[which], 4 * b)
                for c in range(C):
                    dve.bn_aggr(mean_var[which][:, c, :], stats[which][:, c, :]).then_inc(aggr_done[which], 1)

            def lo_half(b, i, bank):
                which, m = QK_ORDER[i]
                wait(dve, hi_ready, 4 * b + i + 1)
                dve.scalar_tensor_tensor(lo[:, which, m, :], misc[bank][:, :], bqk[:, which, m:m + 1],
                                         hi[:, which, m, :].bitcast(F32), ALU.add,
                                         ALU.subtract).then_inc(lo_ready, 1)

            def rest(dst, src, hi_part, done):
                dve.tensor_tensor(dst, src, hi_part.bitcast(F32), ALU.subtract).then_inc(done, 1)

            def xT_rest(b, f, bank):
                wait(dve, xT_hi, 2 * b + f + 1)
                wait(dve, qk_done, 4 * b)
                wait(dve, z_done, 2 * (b - 2))
                rest(normedT_lo[:, f, :], misc[bank][:, :], normedT_hi[:, f, :], xT_ready)

            def yT_rest(b, f, bank, prep):
                wait(dve, yT_hi, 2 * b + f + 1)
                wait(dve, qk_done, 4 * (b + 2) if prep else 0)
                wait(dve, z_done, 2 * b)
                rest(normedT_lo[:, f, :], misc[bank][:, :], normedT_hi[:, f, :], yT_ready)

            def w21_rest(b):
                wait(dve, w21_hi_ready, 2 * b + 2)
                wait(dve, z_done, 2 * b)
                dve.tensor_tensor(w21_lo[:, 0, :], w21_half[:, :], w21_hi[:, 0, :].bitcast(F32), ALU.subtract)
                rest(w21_lo[:, 1, :], misc[0][:, 0:D], w21_hi[:, 1, :], w21_ready)

            def w_rest(w):
                wait(dve, w_hi_ready, (WK, WQ, WV, WO).index(w) + 1)
                dve.scalar_tensor_tensor(w_lo[:, w], w_in[:, w], SCALE if w == WQ else 1.0,
                                         w_hi[:, w].bitcast(F32), ALU.mult, ALU.subtract).then_inc(w_ready, 1)

            def v_copy(b, half, bank):
                wait(dve, v_done, 2 * b + half + 1)
                wait(dve, v_stacked, 4 * b)
                dve.tensor_tensor(v_nat[:, 2 * half:2 * half + 2, :],
                                  misc[bank][:, :].rearrange("p (c d) -> p c d", c=2), bv_all[:, :, :].to_broadcast([P, 2, D]),
                                  ALU.add).then_inc(v_ready, 1)

            def odd_quad(b, pair):
                n = 2 * b + pair
                wait(dve, odd_copied, n + 1)
                wait(dve, even_masked, n + 1)
                wait(dve, attn_ready, n)
                dve.scalar_tensor_tensor(pair_ctx[:, :], pv_bank[:, :], half_hi[:, 0:1], even_ctx[:, :],
                                         ALU.mult, ALU.add).then_inc(odd_out, 1)

            def invert(b, pair):
                n = 2 * b + pair
                wait_apart(dve, sums_in, 32 * n + 32)
                wait_apart(dve, inv_saved, 32 * n)
                dve.reciprocal(inv_small[:, :], sums[:, :]).then_inc(recip_ready, 1)

            def y_half(b, half, bank):
                wait(dve, wo_done, 2 * b + half + 1)
                wait(dve, xbo_ready, b + 1)
                dve.tensor_tensor(y[:, 2 * half:2 * half + 2, :],
                                  misc[bank][:, :].rearrange("p (c d) -> p c d", c=2),
                                  y[:, 2 * half:2 * half + 2, :], ALU.add).then_inc(y_ready, 1)
                wait(dve, y_ready, 2 * b + half + 1)
                statistics(1, b, y, 2 * half, 2 * half + 2)

            def out_half(b, half, bank):
                wait(dve, z_done, 2 * b + half + 1)
                wait(dve, yb_ready, b + 1)
                dve.tensor_tensor(y[:, 2 * half:2 * half + 2, :],
                                  misc[bank][:, :].rearrange("p (c d) -> p c d", c=2),
                                  y[:, 2 * half:2 * half + 2, :], ALU.add).then_inc(out_ready, 1)

            def turn(b, post, prep, load):
                for u in range(UNITS):
                    for row, n in nats_of(b, u, post, prep):
                        row_max(row, n)
                    u0, row = (0, b + 1) if not post else (None, None)
                    if u >= 56 and load:
                        u0, row = 56, b + 2
                    if u0 is not None:
                        if u == u0:
                            wait(dve, x_loaded, 16 * (row + 1))
                        if u in (u0, u0 + 1):
                            c = 2 * (u - u0)
                            statistics(0, row, x_in, c, c + 2)
                        if u == u0 + 2:
                            aggregate(0, row)
                    if post:
                        if u == 3:
                            odd_quad(b - 1, 1)
                        if u == 11:
                            invert(b - 1, 1)
                    if prep and u in (3, 5):
                        v_copy(b + 1, (u - 3) // 2, (5 - u) // 2)
                    if post and u == 1:
                        w21_rest(b - 1)
                    if u == 8:
                        max_halves(b, 1, 1)
                    if prep and u in (13, 14):
                        xT_rest(b + 1, u - 13, 14 - u)
                    if post and u in (38, 41):
                        f = (u - 38) // 3
                        yT_rest(b - 1, f, f, prep)
                    if prep and u in HALF_UNITS:
                        i = HALF_UNITS.index(u)
                        lo_half(b + 1, i, QK_BANKS[i])
                    if u == 24:
                        max_halves(b, 2, 0)
                    if post:
                        if u in (26, 29):
                            half = (u - 26) // 3
                            y_half(b - 1, half, 1 - half)
                        if u == 30:
                            aggregate(1, b - 1)
                    if u == 35:
                        odd_quad(b, 0)
                    if u == 41:
                        max_halves(b, 3, 0)
                    if post and u in (46, 49):
                        half = (u - 46) // 3
                        out_half(b - 1, half, half)
                    if u == 44:
                        invert(b, 0)
                    if u == 55 and prep:
                        max_halves(b + 1, 0, 1)

            dve.memset(ones[:, :], 1.0).then_inc(dve_set, 1)
            dve.memset(ks[ZROW:MROW, 0:8, :].bitcast(F32), 0.0).then_inc(dve_set, 1)
            dve.wait_ge(pool_set, 3)
            halves = ident[:, :].rearrange("p (j h d) -> p h j d", j=4, h=2)
            dve.tensor_reduce(half_lo[:, :], halves[:, 0], AX.XY, ALU.add).then_inc(dve_set, 1)
            dve.tensor_reduce(half_hi[:, :], halves[:, 1], AX.XY, ALU.add).then_inc(dve_set, 1)
            dve.wait_ge(x_loaded, 16)
            statistics(0, 0, x_in, 0, 4)
            aggregate(0, 0)
            dve.tensor_copy(pick[:, :, 0], halves[:, 1, :, 0])
            dve.tensor_copy(pick[:, :, 1], halves[:, 0, :, 0]).then_inc(dve_set, 1)
            w_rest(WK)
            dve.wait_ge(ctx_hi_ready, 1)
            rest(ctx_lo[:, :, :], ctx_in[:, :, :], ctx_hi[:, :, :], ctx_ready)
            w_rest(WQ)
            dve.wait_ge(act_set, 2)
            lo_half(0, 0, FIRST_BANKS[0])
            for f in range(F):
                xT_rest(0, f, 2 + f)
            lo_half(0, 1, FIRST_BANKS[1])
            w_rest(WV)
            lo_half(0, 2, FIRST_BANKS[2])
            w_rest(WO)
            lo_half(0, 3, FIRST_BANKS[3])
            v_copy(0, 0, 6)
            v_copy(0, 1, 7)
            for n in range(FIRST_LEAD):
                row_max(0, n)
                if n == 18:
                    max_halves(0, 0, 0)
            turns(dve, turn)
            dve.wait_ge(pv_done, 16 * B)
            dve.wait_ge(last_even, 1)
            dve.scalar_tensor_tensor(odd_sum[:, :], pv_bank[:, :], half_lo[:, 0:1], odd_sum[:, :],
                                     ALU.mult, ALU.add).then_inc(last_comb, 1)
            dve.wait_ge(even_masked, 2 * B)
            dve.wait_ge(attn_ready, 2 * LAST + 1)
            dve.scalar_tensor_tensor(pair_ctx[:, :], pv_bank[:, :], half_hi[:, 0:1], even_ctx[:, :],
                                     ALU.mult, ALU.add).then_inc(odd_out, 1)
            dve.wait_ge(last_sums, 1)
            dve.wait_ge(inv_saved, 32 * (2 * LAST + 1))
            dve.reciprocal(inv_small[:, :], misc[LAST_SUMS_BANK][:, 0:32]).then_inc(recip_ready, 1)
            dve.wait_ge(recip_ready, 2 * B)
            dve.tensor_copy(even_sum[:, :].rearrange("p (k i) -> p k i", i=HD),
                            inv_small[:, :].unsqueeze(2).to_broadcast([P, 32, HD])).then_inc(last_recip, 1)
            w21_rest(LAST)
            dve.wait_ge(last_inv, 1)
            dve.wait_ge(odd_out, 2 * B)
            dve.wait_ge(wo_done, 2 * LAST)
            dve.tensor_tensor(pair_ctx[:, :], pair_ctx[:, :], misc[LAST_INV_BANK][:, :],
                              ALU.mult).then_inc(divided, 1)
            dve.wait_ge(attn_hi_ready, 2 * B)
            rest(attnT_lo[:, 1, :], pair_ctx[:, :], attnT_hi[:, 1, :], last_attn)
            dve.wait_ge(xbo_ready, B)
            dve.wait_ge(aggr_done[1], 4 * LAST)
            for c in range(C):
                dve.wait_ge(last_wo, c + 1)
                dve.tensor_tensor(y[:, c, :], misc[LAST_WO_BANKS[c]][:, 0:D], y[:, c, :],
                                  ALU.add).then_inc(last_y, 1)
                dve.wait_ge(last_y, c + 1)
                dve.bn_stats(stats[1][:, c, :], y[:, c, :]).then_inc(stat_done[1], 1)
            aggregate(1, LAST)
            dve.wait_ge(root_step[1], 3 * LAST + 2)
            dve.wait_ge(yT_done, 2 * LAST)
            for c in range(3):
                dve.tensor_scalar(normed[:, c, :], y[:, c, :], mean_var[1][:, c, 0:1], rstd[1][:, c:c + 1],
                                  ALU.subtract, ALU.mult).then_inc(last_norm, 1)
            for f in range(F):
                yT_rest(LAST, f, LAST_YT_BANKS[f], False)
            for c in range(C):
                dve.wait_ge(last_z, c + 1)
                last = dve.tensor_tensor(y[:, c, :], misc[LAST_Z_BANKS[c]][:, 0:D], y[:, c, :], ALU.add)
                if c % 2:
                    last.then_inc(out_ready, 1)

        @block.gpsimd
        def _(pool):
            def inverse_root(which, b):
                wait(pool, aggr_done[which], 4 * b + 4)
                wait_apart(pool, norm_ready[which], 4 * b)
                pool.tensor_scalar(var_eps[which][:, :], mean_var[which][:, :, 1], EPS, None,
                                   ALU.add).then_inc(root_step[which], 1)
                wait(pool, root_step[which], 3 * b + 1)
                pool.tensor_tensor(rstd[which][:, :], var_eps[which][:, :], neg_half[:, :],
                                   ALU.pow).then_inc(root_step[which], 1)
                wait(pool, root_step[which], 3 * b + 2)
                pool.tensor_tensor(shift[which][:, :], mean_var[which][:, :, 0], rstd[which][:, :],
                                   ALU.mult).then_inc(root_step[which], 1)
                wait_apart(pool, root_step[which], 3 * b + 3)
                pool.tensor_scalar(shift[which][:, :], shift[which][:, :], -1.0, None,
                                   ALU.mult).then_inc(rstd_ready[which], 1)

            def v_stack(b, g):
                wait(pool, v_ready, 2 * b + 2)
                wait_apart(pool, pv_done, 16 * (b - 1) + 4 * g + 4)
                at = 16 * (g % 2)
                pool.tensor_copy(vs[:, :, 4 * g:4 * g + 4, at:at + 16],
                                 v_nat[:, :, 64 * g:64 * g + 64].rearrange("p c (h d) -> p c h d", h=4))\
                    .then_inc(v_stacked, 1)

            def divide(b, pair):
                n = 2 * b + pair
                wait(pool, inv_ready, 16 * n + 16)
                wait(pool, odd_out, n + 1)
                pool.tensor_tensor(pair_ctx[:, :], pair_ctx[:, :], inv_sum[:, :], ALU.mult).then_inc(divided, 1)

            def attn_rest(b, pair):
                n = 2 * b + pair
                wait(pool, attn_hi_ready, n + 1)
                pool.tensor_tensor(attnT_lo[:, pair, :], pair_ctx[:, :], attnT_hi[:, pair, :].bitcast(F32),
                                   ALU.subtract).then_inc(attn_ready, 1)

            def ctx_rest(b):
                wait(pool, ctx_hi_ready, b + 1)
                pool.tensor_tensor(ctx_lo[:, :, :], ctx_in[:, :, :], ctx_hi[:, :, :].bitcast(F32),
                                   ALU.subtract).then_inc(ctx_ready, 1)

            def add_bo(b):
                wait(pool, y_loaded, 16 * (b + 1))
                for c in range(C):
                    last = pool.tensor_tensor(y[:, c, :], y[:, c, :], bo_all[:, :], ALU.add)
                last.then_inc(xbo_ready, 1)

            def add_b2(b):
                wait(pool, norm_ready[1], 4 * b + 4)
                wait(pool, b2_ready, b + 1)
                for c in range(C):
                    last = pool.tensor_tensor(y[:, c, :], y[:, c, :], b2_all[:, :], ALU.add)
                last.then_inc(yb_ready, 1)

            def b2_parts(b):
                wait(pool, ffn_loaded, 64 * (b + 1))
                wait(pool, b2_done, b)
                pool.tensor_tensor(b2_part[:, 0:4, :], w2_in[:, 0:4, :],
                                   b1_in[:, 0:4].unsqueeze(2).to_broadcast([P, 4, D]),
                                   ALU.mult).then_inc(b2_step, 1)
                for k in range(4):
                    wait(pool, b2_step, B2_STEPS * b + 2 * k + 1)
                    pool.tensor_tensor(b2_part[:, 4, :], w2_in[:, 4 + k, :],
                                       b1_in[:, 4 + k:5 + k].to_broadcast([P, D]), ALU.mult).then_inc(b2_step, 1)
                    wait(pool, b2_step, B2_STEPS * b + 2 * k + 2)
                    pool.tensor_tensor(b2_part[:, k, :], b2_part[:, k, :], b2_part[:, 4, :],
                                       ALU.add).then_inc(b2_step, 1)
                for k, width in enumerate((2, 1)):
                    wait(pool, b2_step, B2_STEPS * b + k + 9)
                    pool.tensor_tensor(b2_part[:, 0:width, :], b2_part[:, 0:width, :],
                                       b2_part[:, width:2 * width, :], ALU.add).then_inc(b2_step, 1)
                wait(pool, b2_step, B2_STEPS * b + B2_STEPS)
                pool.tensor_tensor(b2_part[0:1, 0, :], b2_part[0:1, 0, :], b2_in[:, :],
                                   ALU.add).then_inc(b2_part_ready, 1)

            def turn(b, post, prep, load):
                if not post:
                    inverse_root(0, b + 1)
                if post:
                    v_stack(b, 3)
                    divide(b - 1, 1)
                if prep:
                    v_stack(b + 1, 0)
                if post:
                    attn_rest(b - 1, 1)
                    inverse_root(1, b - 1)
                    add_b2(b - 1)
                if prep:
                    v_stack(b + 1, 1)
                if load:
                    ctx_rest(b + 2)
                b2_parts(b)
                divide(b, 0)
                attn_rest(b, 0)
                if prep:
                    v_stack(b + 1, 2)
                if load:
                    inverse_root(0, b + 2)
                add_bo(b)

            pool.memset(ident[:, :], 0.0).then_inc(pool_set, 1)
            pool.memset(neg_half[:, :], -0.5).then_inc(pool_set, 1)
            pool.wait_ge(pool_set, 1)
            pool.affine_select(out=ident[:, :], in_=ident[:, :], compare_op=ALU.not_equal, fill=1.0, base=0,
                               pattern=[[-1, P]], channel_multiplier=1).then_inc(pool_set, 1)
            pool.wait_ge(pool_set, 3)
            pool.memset(qs[ZROW:MROW, 0:8, :].bitcast(F32), 0.0).then_inc(rows_set, 1)
            pool.wait_ge(rows_set, 1)
            inverse_root(0, 0)
            pool.wait_ge(rstd_ready[0], 1)
            pool.memset(qs[ZROW:MROW, 8:H, :].bitcast(F32), 0.0).then_inc(rows_set, 1)
            pool.wait_ge(rows_set, 2)
            pool.memset(vs[:, :, :, :], 1.0).then_inc(rows_set, 1)
            pool.wait_ge(rows_set, 3)
            pool.memset(ks[MROW:KS, :, :].bitcast(F32), 1.0).then_inc(rows_set, 1)
            pool.wait_ge(rows_set, 4)
            pool.wait_ge(const_in, CONSTS)
            for g in range(QUADS):
                v_stack(0, g)
            ctx_rest(1)
            turns(pool, turn)
            inverse_root(1, LAST)


def kernel(**inputs):
    import numpy as np
    import concourse.bacc as bacc
    from concourse.bass_utils import run_bass_kernel_spmd

    a = {k: np.asarray(v) for k, v in inputs.items()}
    def by_quad(w):
        return w.reshape((2, 2, 4, HD) + w.shape[1:]).swapaxes(2, 3).reshape(w.shape)

    wo_rows = a["L0_xattn_Wo"].T.reshape(2, 2, 4, HD, D).transpose(0, 2, 1, 3, 4).reshape(D, D)
    arrays = {
        "x": a["x"],
        "ctxT": a["ctx_1024"].transpose(0, 2, 1).reshape(B, F, P, S),
        "wqT": by_quad(a["L0_xattn_Wq"]).T,
        "bq": by_quad(a["L0_xattn_bq"]).reshape(2, P).T,
        "wkT": by_quad(a["L0_xattn_Wk"]).T,
        "bk": by_quad(a["L0_xattn_bk"]).reshape(2, P).T,
        "wvT": a["L0_xattn_Wv"].T,
        "bv": a["L0_xattn_bv"],
        "woT": wo_rows,
        "bo": a["L0_xattn_bo"],
        "w1": a["L0_ffn_W1"],
        "b1": a["L0_ffn_b1"],
        "w2T": a["L0_ffn_W2"].transpose(0, 2, 1),
        "b2": a["L0_ffn_b2"],
    }
    nc = bacc.Bacc("TRN2", target_bir_lowering=False, num_devices=1)
    arrays = {k: np.ascontiguousarray(v) for k, v in arrays.items()}
    args = [nc.dram_tensor(k, v.shape, mybir.dt.from_np(v.dtype), kind="ExternalInput").ap()
            for k, v in arrays.items()]
    args.append(nc.dram_tensor("out", (B, S, D), F32, kind="ExternalOutput").ap())
    xattn_ffn(nc, *args)
    r = run_bass_kernel_spmd(nc, [arrays], core_ids=[0])
    return r.results[0]["out"]
```
